# Optimizing a Trainium2 kernel written in Bass

```python
import numpy as np
import jax
import jax.numpy as jnp

def _softmax(x, axis=-1):
    return jax.nn.softmax(x, axis=axis)

def _gelu(x):
    return jax.nn.gelu(x, approximate=True)

def _silu(x):
    return jax.nn.silu(x)

def _sigmoid(x):
    return jax.nn.sigmoid(x)

def _layernorm(x, axis=-1, eps=1e-05):
    m = jnp.mean(x, axis=axis, keepdims=True)
    v = jnp.var(x, axis=axis, keepdims=True)
    return (x - m) / jnp.sqrt(v + eps)

def _scatter_add(tgt, idx, src, axis=0):
    return tgt.at[idx].add(src)

def _segment_sum(src, seg, n):
    return jax.ops.segment_sum(src, seg, n)
kernel_name = 'mk_seq_postln_d1_jaxref_r8_e4ae38'

def setup_inputs(seed: int=0):
    np.random.seed(seed)
    _w = jnp.asarray

    def _L0_attn_setup():
        import jax, jax.numpy as jnp
        import numpy as np
        D_MODEL = 512
        D_XB = 128
        D_INNER = 512
        HEADDIM = 128
        DSTATE = 128
        NHEADS = D_INNER // HEADDIM
        DCONV = 4
        INTER = 1792
        EPS = 1e-05
        CHUNK = 128

        def rmsnorm(x, w):
            return x * jax.lax.rsqrt(jnp.mean(x * x, axis=-1, keepdims=True) + EPS) * w

        def silu(x):
            return x * jax.nn.sigmoid(x)

        def mamba2(x, w_in, conv_w, conv_b, A_log, D, dt_bias, w_out):
            B, L, _ = x.shape
            H, P, N = (NHEADS, HEADDIM, DSTATE)
            G = D_XB // P
            rep = H // G
            zxbcdt = x @ w_in.T
            z, xs, Bs, Cs, dt = jnp.split(zxbcdt, [D_INNER, D_INNER + D_XB, D_INNER + 2 * D_XB, 2 * D_INNER + 2 * D_XB], axis=-1)
            xBC = jnp.concatenate([xs, Bs, Cs], axis=-1)
            conv = jax.lax.conv_general_dilated(xBC.transpose(0, 2, 1), conv_w[:, None, :], (1,), [(DCONV - 1, 0)], feature_group_count=conv_w.shape[0])
            xBC = silu(conv.transpose(0, 2, 1) + conv_b)
            xs, Bs, Cs = jnp.split(xBC, [D_XB, 2 * D_XB], axis=-1)
            dt = jax.nn.softplus(dt + dt_bias)
            A = -jnp.exp(A_log)
            xh = jnp.repeat(xs.reshape(B, L, G, P), rep, axis=2)
            Bh = jnp.repeat(Bs.reshape(B, L, G, N), rep, axis=2)
            Ch = Cs.reshape(B, L, H, N)
            c, Q = (L // CHUNK, CHUNK)
            a = (dt * A).reshape(B, c, Q, H).transpose(0, 1, 3, 2)
            dtc = dt.reshape(B, c, Q, H).transpose(0, 1, 3, 2)
            Xc = xh.reshape(B, c, Q, H, P).transpose(0, 1, 3, 2, 4)
            Bc = Bh.reshape(B, c, Q, H, N).transpose(0, 1, 3, 2, 4)
            Cc = Ch.reshape(B, c, Q, H, N).transpose(0, 1, 3, 2, 4)
            cs = jnp.cumsum(a, axis=-1)
            tri = jnp.tril(jnp.ones((Q, Q), bool))
            Ldec = jnp.where(tri, jnp.exp(cs[..., :, None] - cs[..., None, :]), 0.0)
            Xdt = Xc * dtc[..., None]
            att = jnp.einsum('bchqn,bchkn->bchqk', Cc, Bc) * Ldec
            Yd = jnp.einsum('bchqk,bchkp->bchqp', att, Xdt)
            dec_end = jnp.exp(cs[..., -1:] - cs)
            states = jnp.einsum('bchq,bchqn,bchqp->bchpn', dec_end, Bc, Xdt)
            g = jnp.exp(cs[..., -1])

            def step(S, inp):
                gk, st = inp
                return (gk[:, :, None, None] * S + st, S)
            S0 = jnp.zeros((B, H, P, N), x.dtype)
            _, prev = jax.lax.scan(step, S0, (g.transpose(1, 0, 2), states.transpose(1, 0, 2, 3, 4)))
            prev = prev.transpose(1, 0, 2, 3, 4)
            Yo = jnp.einsum('bchqn,bchpn,bchq->bchqp', Cc, prev, jnp.exp(cs))
            Y = (Yd + Yo).transpose(0, 1, 3, 2, 4).reshape(B, L, H, P)
            Y = Y + D[:, None] * xh
            y = Y.reshape(B, L, D_INNER) * silu(z)
            return y @ w_out.T
        key = jax.random.key(seed)
        ks = jax.random.split(key, 10)
        B, L = (2, 256)
        proj_out = 2 * D_INNER + 2 * D_XB + NHEADS
        conv_dim = 2 * D_XB + D_INNER
        return {'hidden_states': jax.random.normal(ks[0], (B, L, D_MODEL), jnp.float32), 'w_in': jax.random.normal(ks[1], (proj_out, D_MODEL), jnp.float32) * 0.02, 'conv_w': jax.random.normal(ks[2], (conv_dim, DCONV), jnp.float32) * 0.1, 'conv_b': jnp.zeros((conv_dim,), jnp.float32), 'A_log': jnp.log(jnp.arange(1, NHEADS + 1, dtype=jnp.float32)), 'D': jnp.ones((NHEADS,), jnp.float32), 'dt_bias': jax.random.normal(ks[3], (NHEADS,), jnp.float32) * 0.1, 'w_out': jax.random.normal(ks[4], (D_MODEL, D_INNER), jnp.float32) * 0.02, 'ln1_w': jnp.ones((D_MODEL,), jnp.float32), 'ln2_w': jnp.ones((D_MODEL,), jnp.float32), 'gate_w': jax.random.normal(ks[5], (INTER, D_MODEL), jnp.float32) * 0.02, 'up_w': jax.random.normal(ks[6], (INTER, D_MODEL), jnp.float32) * 0.02, 'down_w': jax.random.normal(ks[7], (D_MODEL, INTER), jnp.float32) * 0.02}
    _L0_attn_in = _L0_attn_setup()

    def _L0_ffn_setup():
        import jax, jax.numpy as jnp
        import numpy as np
        D = 512
        F = 1376
        B, S = (4, 256)
        key = jax.random.key(seed)
        k_x, k_g, k_u, k_d = jax.random.split(key, 4)
        scale = 0.02
        return {'x': jax.random.normal(k_x, (B, S, D), dtype=jnp.float32), 'W_gate': jax.random.normal(k_g, (F, D), dtype=jnp.float32) * scale, 'W_up': jax.random.normal(k_u, (F, D), dtype=jnp.float32) * scale, 'W_down': jax.random.normal(k_d, (D, F), dtype=jnp.float32) * scale}
    _L0_ffn_in = _L0_ffn_setup()
    _d = {'L0_attn_hidden_states': _L0_attn_in['hidden_states'], 'L0_attn_w_in': _L0_attn_in['w_in'], 'L0_attn_conv_w': _L0_attn_in['conv_w'], 'L0_attn_conv_b': _L0_attn_in['conv_b'], 'L0_attn_A_log': _L0_attn_in['A_log'], 'L0_attn_D': _L0_attn_in['D'], 'L0_attn_dt_bias': _L0_attn_in['dt_bias'], 'L0_attn_w_out': _L0_attn_in['w_out'], 'L0_attn_ln1_w': _L0_attn_in['ln1_w'], 'L0_attn_ln2_w': _L0_attn_in['ln2_w'], 'L0_attn_gate_w': _L0_attn_in['gate_w'], 'L0_attn_up_w': _L0_attn_in['up_w'], 'L0_attn_down_w': _L0_attn_in['down_w'], 'L0_ffn_W_gate': _L0_ffn_in['W_gate'], 'L0_ffn_W_up': _L0_ffn_in['W_up'], 'L0_ffn_W_down': _L0_ffn_in['W_down']}
    _x0 = _d['L0_attn_hidden_states']
    _d['L0_attn_hidden_states'] = jax.random.normal(jax.random.fold_in(jax.random.key(seed), 1), (1, 1024, 512), dtype=_x0.dtype)
    del _x0
    return _d

def reference(L0_attn_hidden_states, L0_attn_w_in, L0_attn_conv_w, L0_attn_conv_b, L0_attn_A_log, L0_attn_D, L0_attn_dt_bias, L0_attn_w_out, L0_attn_ln1_w, L0_attn_ln2_w, L0_attn_gate_w, L0_attn_up_w, L0_attn_down_w, L0_ffn_W_gate, L0_ffn_W_up, L0_ffn_W_down):

    def _L0_attn_ref(hidden_states, w_in, conv_w, conv_b, A_log, D, dt_bias, w_out, ln1_w, ln2_w, gate_w, up_w, down_w):
        import jax, jax.numpy as jnp
        import numpy as np
        D_MODEL = 512
        D_XB = 128
        D_INNER = 512
        HEADDIM = 128
        DSTATE = 128
        NHEADS = D_INNER // HEADDIM
        DCONV = 4
        INTER = 1792
        EPS = 1e-05
        CHUNK = 128

        def rmsnorm(x, w):
            return x * jax.lax.rsqrt(jnp.mean(x * x, axis=-1, keepdims=True) + EPS) * w

        def silu(x):
            return x * jax.nn.sigmoid(x)

        def mamba2(x, w_in, conv_w, conv_b, A_log, D, dt_bias, w_out):
            B, L, _ = x.shape
            H, P, N = (NHEADS, HEADDIM, DSTATE)
            G = D_XB // P
            rep = H // G
            zxbcdt = x @ w_in.T
            z, xs, Bs, Cs, dt = jnp.split(zxbcdt, [D_INNER, D_INNER + D_XB, D_INNER + 2 * D_XB, 2 * D_INNER + 2 * D_XB], axis=-1)
            xBC = jnp.concatenate([xs, Bs, Cs], axis=-1)
            conv = jax.lax.conv_general_dilated(xBC.transpose(0, 2, 1), conv_w[:, None, :], (1,), [(DCONV - 1, 0)], feature_group_count=conv_w.shape[0])
            xBC = silu(conv.transpose(0, 2, 1) + conv_b)
            xs, Bs, Cs = jnp.split(xBC, [D_XB, 2 * D_XB], axis=-1)
            dt = jax.nn.softplus(dt + dt_bias)
            A = -jnp.exp(A_log)
            xh = jnp.repeat(xs.reshape(B, L, G, P), rep, axis=2)
            Bh = jnp.repeat(Bs.reshape(B, L, G, N), rep, axis=2)
            Ch = Cs.reshape(B, L, H, N)
            c, Q = (L // CHUNK, CHUNK)
            a = (dt * A).reshape(B, c, Q, H).transpose(0, 1, 3, 2)
            dtc = dt.reshape(B, c, Q, H).transpose(0, 1, 3, 2)
            Xc = xh.reshape(B, c, Q, H, P).transpose(0, 1, 3, 2, 4)
            Bc = Bh.reshape(B, c, Q, H, N).transpose(0, 1, 3, 2, 4)
            Cc = Ch.reshape(B, c, Q, H, N).transpose(0, 1, 3, 2, 4)
            cs = jnp.cumsum(a, axis=-1)
            tri = jnp.tril(jnp.ones((Q, Q), bool))
            Ldec = jnp.where(tri, jnp.exp(cs[..., :, None] - cs[..., None, :]), 0.0)
            Xdt = Xc * dtc[..., None]
            att = jnp.einsum('bchqn,bchkn->bchqk', Cc, Bc) * Ldec
            Yd = jnp.einsum('bchqk,bchkp->bchqp', att, Xdt)
            dec_end = jnp.exp(cs[..., -1:] - cs)
            states = jnp.einsum('bchq,bchqn,bchqp->bchpn', dec_end, Bc, Xdt)
            g = jnp.exp(cs[..., -1])

            def step(S, inp):
                gk, st = inp
                return (gk[:, :, None, None] * S + st, S)
            S0 = jnp.zeros((B, H, P, N), x.dtype)
            _, prev = jax.lax.scan(step, S0, (g.transpose(1, 0, 2), states.transpose(1, 0, 2, 3, 4)))
            prev = prev.transpose(1, 0, 2, 3, 4)
            Yo = jnp.einsum('bchqn,bchpn,bchq->bchqp', Cc, prev, jnp.exp(cs))
            Y = (Yd + Yo).transpose(0, 1, 3, 2, 4).reshape(B, L, H, P)
            Y = Y + D[:, None] * xh
            y = Y.reshape(B, L, D_INNER) * silu(z)
            return y @ w_out.T
        res = hidden_states
        h = rmsnorm(hidden_states, ln1_w)
        h = res + mamba2(h, w_in, conv_w, conv_b, A_log, D, dt_bias, w_out)
        res = h
        h2 = rmsnorm(h, ln2_w)
        mlp = silu(h2 @ gate_w.T) * (h2 @ up_w.T) @ down_w.T
        return res + mlp

    def _L0_ffn_ref(x, W_gate, W_up, W_down):
        import jax, jax.numpy as jnp
        import numpy as np
        D = 512
        F = 1376
        B, S = (4, 256)
        out_shape = x.shape[:-1] + (W_down.shape[0],)
        xt = x.reshape(-1, x.shape[-1])
        up = xt @ W_up.T
        gate = jax.nn.silu(xt @ W_gate.T)
        y = gate * up @ W_down.T
        return y.reshape(out_shape)
    x = L0_attn_hidden_states
    x = _layernorm(x + _L0_attn_ref(x, L0_attn_w_in, L0_attn_conv_w, L0_attn_conv_b, L0_attn_A_log, L0_attn_D, L0_attn_dt_bias, L0_attn_w_out, L0_attn_ln1_w, L0_attn_ln2_w, L0_attn_gate_w, L0_attn_up_w, L0_attn_down_w), axis=-1)
    x = _layernorm(x + _L0_ffn_ref(x, L0_ffn_W_gate, L0_ffn_W_up, L0_ffn_W_down), axis=-1)
    return x

_drawn_inputs = setup_inputs


def setup_inputs(seed=0):
    import zlib

    import numpy as np

    out = dict(_drawn_inputs(seed))
    spreads = {'L0_attn_conv_b': (0.0, 0.8),
     'L0_attn_D': (1.0, 0.6),
     'L0_attn_ln1_w': (1.0, 0.6),
     'L0_attn_ln2_w': (1.0, 0.6)}
    factors = {'L0_attn_w_in': 8.0,
     'L0_attn_conv_w': 8.0,
     'L0_attn_A_log': 8.0,
     'L0_attn_dt_bias': 8.0,
     'L0_attn_w_out': 7.34,
     'L0_attn_gate_w': 64.0,
     'L0_attn_up_w': 64.0,
     'L0_attn_down_w': 64.0}
    for name, (base, spread) in spreads.items():
        noise = np.random.default_rng([zlib.crc32(name.encode()), seed]).standard_normal(out[name].shape)
        drawn = base * np.exp(spread * noise) if base else spread * noise
        out[name] = jnp.asarray(drawn.astype(out[name].dtype))
    for name, factor in factors.items():
        out[name] = (out[name] * factor).astype(out[name].dtype)
    return out
```

```python
from contextlib import ExitStack

import numpy as np

import concourse.bass as bass
from concourse import mybir

F32 = mybir.dt.float32
F32R = mybir.dt.float32r
ALU = mybir.AluOpType
ACT = mybir.ActivationFunctionType

P = 128
L = 1024
DM = 512
KT = DM // P
H = 4
NCH = L // P
NHALF = 2
CPH = NCH // NHALF
HT = L // NHALF
TAPS = 4
HALO = TAPS - 1
CONV = 6
EPS = 1e-5
F_MLP, F_FFN = 1792, 1376
T_MLP = F_MLP // P
T_FFN = -(-F_FFN // P)
IN_TILES = [("dt", 0), ("conv", 1), ("conv", 0), ("conv", 2), ("conv", 3), ("conv", 4),
            ("conv", 5), ("z", 0), ("z", 1), ("z", 2), ("z", 3), ("pad", 0)]
IN_PAIRS = len(IN_TILES) // 2
STAGES = [(IN_PAIRS, H, T_MLP, 0), (IN_PAIRS, H, T_MLP, 1),
          (IN_PAIRS + T_MLP, H + T_MLP, T_FFN, 0), (IN_PAIRS + T_MLP, H + T_MLP, T_FFN, 1)]
BASE = [0, T_MLP, 2 * T_MLP, 2 * T_MLP + T_FFN]
STEPS = 2 * (T_MLP + T_FFN)
U0 = NHALF * IN_PAIRS
CONSTS = 6
SOFT_STEPS = 19
CONV_ORDER = [j for kind, j in IN_TILES if kind == "conv"]
IN_COUNT = len(IN_TILES) - 1
ATANH = [1.0 / (2 * n + 1) for n in range(8)]


def build(nc, x, pairs, downs, conv_w, conv_b, a_log, d_skip, dt_bias, ln1, ln2, out):
    ctx = ExitStack()
    with ctx:
        def sb(name, shape, dt=F32):
            return ctx.enter_context(nc.sbuf_tensor(name, shape, dt))

        def sem(name):
            return ctx.enter_context(nc.semaphore(name))

        resid = sb("resid", [P, NCH, DM])
        act_hi = sb("act_hi", [P, NHALF, KT, HT], F32R)
        act_lo = sb("act_lo", [P, NHALF, KT, HT], F32R)
        zs = sb("zs", [P, NHALF, H, HT])
        cin = sb("cin", [P, CONV, HALO + HT])
        xbc = sb("xbc", [P, NHALF, CONV, HT])
        wo_hi = sb("wo_hi", [P, H, DM], F32R)
        wo_lo = sb("wo_lo", [P, H, DM], F32R)
        pair_raw = sb("pair_raw", [P, 2, 2, KT, P])
        pair_hi = sb("pair_hi", [P, 2, 2, KT, P], F32R)
        pair_lo = sb("pair_lo", [P, 2, 2, KT, P], F32R)
        down_raw = sb("down_raw", [P, 2, DM])
        down_hi = sb("down_hi", [P, 2, DM], F32R)
        down_lo = sb("down_lo", [P, 2, DM], F32R)

        ident = sb("ident", [P, P])
        tri = sb("tri", [P, P])
        strict_f = sb("strict_f", [P, P])
        strict = sb("strict", [P, P], F32R)
        ones = sb("ones", [P, P], F32R)
        ln_b = sb("ln_b", [P, DM])
        dskip_b = sb("dskip_b", [P, H])
        dskip_diag = sb("dskip_diag", [P, H, P])
        dtb_b = sb("dtb_b", [P, H])
        neg_a = sb("neg_a", [P, H])
        cw = sb("cw", [P, CONV, TAPS])
        cb = sb("cb", [P, CONV])
        half_neg = sb("half_neg", [P, 1])

        dt_row = sb("dt_row", [P, HT])
        dv = sb("dv", [P, 6, CPH, H])
        dt_c = sb("dt_c", [P, NHALF, CPH, H])
        a_c = sb("a_c", [P, CPH, H])
        a_hl = sb("a_hl", [P, NHALF, CPH, 2, H], F32R)

        b_hl = sb("b_hl", [P, 2, P], F32R)
        c_hl = sb("c_hl", [P, 2, H, P], F32R)
        bx_hl = sb("bx_hl", [P, 2, 2, P], F32R)
        x_tok = sb("x_tok", [P, P])
        r_hl = sb("r_hl", [P, 2, H, P], F32R)
        decay = sb("decay", [P, H, P])
        carry = sb("carry", [P, H, P])
        carry_last = sb("carry_last", [P, 2, H])
        ce = sb("ce", [P, H, P])
        att = sb("att", [P, H, P])
        att_hl = sb("att_hl", [P, 2, H, P], F32R)
        to_end = sb("to_end", [P, H])
        xs = sb("xs", [P, H, P])
        xs_hl = sb("xs_hl", [P, 2, H, P], F32R)
        state = sb("state", [P, H, P])
        y = sb("y", [P, H, P])
        y_hl = sb("y_hl", [P, 2, H, P], F32R)
        hid = sb("hid", [P, DM])
        normed = sb("normed", [P, 2, DM])
        junk = sb("junk", [P, DM], mybir.dt.bfloat16)
        ssq = sb("ssq", [P, 2, NCH])
        rms = sb("rms", [P, 2, NCH])
        bn = sb("bn", [P, CPH, 6])
        mv = sb("mv", [P, CPH, 2])
        rstd = sb("rstd", [P, CPH])
        gate_s = decay[:, :, :].rearrange("p h q -> p (h q)")
        gated = att[:, :, :].rearrange("p h q -> p (h q)")
        g_hl = [att_hl[:, :, :, :].rearrange("p s h q -> p s (h q)"),
                xs_hl[:, :, :, :].rearrange("p s h q -> p s (h q)")]

        bank = [ctx.enter_context(nc.psum_tensor(f"bank{i}", [P, DM], F32)) for i in range(8)]
        B_IN = bank[0:2]
        B_S, B_D, B_E, B_Y, B_ST, B_O = bank[2:8]
        B_ACC = bank[2:6]
        B_NT = [bank[6], bank[7]]

        def heads(b):
            return b[:, :].rearrange("p (h q) -> p h q", h=H)

        consts_in, ln2_in = sem("consts_in"), sem("ln2_in")
        x_in = [sem(f"x_in{c}") for c in range(NCH)]
        pair_in = [sem(f"pair_in{i}") for i in range(2)]
        down_in = [sem(f"down_in{i}") for i in range(2)]
        zeroed, masks, strict_rdy, ones_rdy, diag_rdy, nega_rdy, aexp_rdy = map(
            sem, ("zeroed", "masks", "strict_rdy", "ones_rdy", "diag_rdy", "nega_rdy", "aexp_rdy"))
        phi, plo, pair_used, dhi, dlo, down_used = map(
            sem, ("pair_hi_rdy", "pair_lo_rdy", "pair_used", "down_hi_rdy", "down_lo_rdy", "down_used"))
        xsq, hsq, ms_rdy, rms_rdy, xn_rdy, xt_ps, xt_hi, xt_lo = map(
            sem, ("xsq", "hsq", "ms_rdy", "rms_rdy", "xn_rdy", "xt_ps", "xt_hi", "xt_lo"))
        in_ps, in_free = sem("in_ps"), sem("in_free")
        cin_rdy, halo_rdy, tap_dve, conv_rdy, b_lo, car_pre = map(
            sem, ("cin_rdy", "halo_rdy", "tap_dve", "conv_rdy", "b_lo", "car_pre"))
        dtt_ps, soft, dt_exp = map(sem, ("dtt_ps", "soft", "dt_exp"))
        cb_hi, cb_lo, bxt_ps, bx_hi, xtok_rdy, bx_lo = map(
            sem, ("cb_hi", "cb_lo", "bxt_ps", "bx_hi", "xtok_rdy", "bx_lo"))
        r_rdy, s_ps, d_ps, e_ps, dec_exp, car_exp, dec_mask, end_rdy, dec_dt = map(
            sem, ("r_rdy", "s_ps", "d_ps", "e_ps", "dec_exp", "car_exp", "dec_mask", "end_rdy", "dec_dt"))
        att_mul, att_d, att_hi_s, att_lo_s, ce_rdy, xs_rdy, xs_hi_s, xs_lo_s = map(
            sem, ("att_mul", "att_d", "att_hi_rdy", "att_lo_rdy", "ce_rdy", "xs_rdy", "xs_hi_rdy", "xs_lo_rdy"))
        y_ps, st_ps, st_rdy, y_rdy, y_hi_s, y_lo_s = map(
            sem, ("y_ps", "st_ps", "state_rdy", "y_rdy", "y_hi_rdy", "y_lo_rdy"))
        o_ps, hid_rdy, hx_rdy, h2_rdy, h2t_ps, h2t_hi, h2t_lo = map(
            sem, ("o_ps", "hid_rdy", "hx_rdy", "h2_rdy", "h2t_ps", "h2t_hi", "h2t_lo"))
        up_ps, gate_ps, silu_rdy, g_rdy, g_hi_s, g_lo_s = map(
            sem, ("up_ps", "gate_ps", "silu_rdy", "g_rdy", "g_hi_rdy", "g_lo_rdy"))
        acc_ps, acc_free, bn_rdy, mv_rdy, ve_rdy, rstd_rdy, ln_rdy, lt_ps, lt_hi, lt_lo = map(
            sem, ("acc_ps", "acc_free", "bn_rdy", "mv_rdy", "ve_rdy", "rstd_rdy", "ln_rdy", "lt_ps", "lt_hi", "lt_lo"))
        out_done = sem("out_done")

        def wait(eng, s, value):
            if not isinstance(value, int) or value > 0:
                eng.wait_ge(s, value)

        block = ctx.enter_context(nc.Block())

        @block.sync
        def _(sp):
            def load_pair(u, tile, slot):
                wait(sp, plo, u - 1)
                sp.dma_start(pair_raw[:, slot, :, :, :], pairs[tile]).then_inc(pair_in[slot], 16)

            def load_down(v, tile, slot):
                wait(sp, dlo, v - 1)
                sp.dma_start(down_raw[:, slot, :], downs[tile]).then_inc(down_in[slot], 16)

            for c in range(CPH):
                sp.dma_start(resid[:, c, :], x[c]).then_inc(x_in[c], 16)
                if c == 0:
                    load_pair(0, 0, 0)
                    sp.dma_start(ln_b[:, :], ln1.to_broadcast([P, DM])).then_inc(consts_in, 16)
            load_pair(1, 1, 1)
            for dst, src in ((cw[:, :, :], conv_w), (cb[:, :], conv_b),
                             (dtb_b[:, :], dt_bias.to_broadcast([P, H])),
                             (neg_a[:, :], a_log.to_broadcast([P, H])),
                             (dskip_b[:, :], d_skip.to_broadcast([P, H]))):
                sp.dma_start(dst, src).then_inc(consts_in, 16)
            for c in range(CPH, NCH):
                sp.dma_start(resid[:, c, :], x[c]).then_inc(x_in[c], 16)
            load_down(0, 0, 0)
            load_down(1, 1, 1)
            for u in range(2, U0 + 2):
                load_pair(u, u % IN_PAIRS if u < U0 else IN_PAIRS + u - U0, u % 2)
                if u == 9:
                    sp.wait_ge(xn_rdy, NCH)
                    sp.dma_start(ln_b[:, :], ln2.to_broadcast([P, DM])).then_inc(ln2_in, 16)
                if u in (7, 8):
                    load_down(u - 5, u - 5, (u - 5) % 2)
            load_down(H, H, 0)

            for s, (p0, d0, n, half) in enumerate(STAGES):
                b = BASE[s]
                looped = (n - 2) // 2
                with sp.Fori(0, looped) as i:
                    for j in range(2):
                        load_pair(i * 2 + (U0 + b + j + 2), i * 2 + (p0 + j + 2), (b + j) % 2)
                        load_down(i * 2 + (H + b + j + 1), i * 2 + (d0 + j + 1), (b + j + 1) % 2)
                for k in range(2 * looped, n):
                    g = b + k
                    following = STAGES[s + 1] if s + 1 < len(STAGES) else None
                    if k + 2 < n:
                        load_pair(U0 + g + 2, p0 + k + 2, g % 2)
                    elif following:
                        load_pair(U0 + g + 2, following[0] + k + 2 - n, g % 2)
                    if k + 1 < n:
                        load_down(H + g + 1, d0 + k + 1, (g + 1) % 2)
                    elif following:
                        load_down(H + g + 1, following[1], (g + 1) % 2)
            for half in range(NHALF):
                for t in range(CPH):
                    wait(sp, ln_rdy, (NHALF + half) * CPH + t + 1)
                    sp.dma_start(out[half * CPH + t], resid[:, half * CPH + t, :]).then_inc(out_done, 16)
            sp.wait_ge(out_done, 16 * NCH)

        @block.gpsimd
        def _(pool):
            for t in (ident, strict_f):
                pool.memset(t[:, :], 0.0).then_inc(zeroed, 1)
            pool.memset(tri[:, :], 1.0).then_inc(zeroed, 1)
            pool.memset(cin[:, :, 0:HALO], 0.0).then_inc(zeroed, 1)
            pool.memset(state[:, :, :], 0.0).then_inc(zeroed, 1)
            pool.memset(half_neg[:, :], -0.5).then_inc(zeroed, 1)
            pool.wait_ge(zeroed, 6)
            pool.affine_select(out=ident[:, :], in_=ident[:, :], compare_op=ALU.not_equal, fill=1.0,
                               base=0, pattern=[[-1, P]], channel_multiplier=1).then_inc(masks, 1)
            pool.affine_select(out=tri[:, :], in_=tri[:, :], compare_op=ALU.is_ge, fill=0.0,
                               base=0, pattern=[[1, P]], channel_multiplier=-1).then_inc(masks, 1)
            pool.affine_select(out=strict_f[:, :], in_=strict_f[:, :], compare_op=ALU.is_ge, fill=1.0,
                               base=0, pattern=[[1, P]], channel_multiplier=-1).then_inc(masks, 1)

            def rms_of(which, n, squares, count):
                pool.wait_ge(squares, count)
                pool.tensor_scalar(rms[:, which, count - 1:count], ssq[:, which, count - 1:count],
                                   1.0 / DM, EPS, ALU.mult, ALU.add).then_inc(ms_rdy, 1)
                pool.wait_ge(ms_rdy, n + 1)
                pool.tensor_tensor(rms[:, which, count - 1:count], rms[:, which, count - 1:count],
                                   half_neg[:, :], ALU.pow).then_inc(rms_rdy, 1)

            for c in range(CPH):
                rms_of(0, c, xsq, c + 1)
            pool.wait_ge(masks, 3)
            pool.wait_ge(consts_in, CONSTS * 16)
            pool.tensor_tensor(dskip_diag[:, :, :],
                               ident[:, :].rearrange("p (a q) -> p a q", a=1).to_broadcast([P, H, P]),
                               dskip_b[:, :].rearrange("p (h a) -> p h a", a=1).to_broadcast([P, H, P]),
                               ALU.mult).then_inc(diag_rdy, 1)
            for c in range(CPH, NCH):
                rms_of(0, c, xsq, c + 1)

            def tri_times_a(n):
                half, c = divmod(n, CPH)
                pool.wait_ge(soft, SOFT_STEPS * (half + 1))
                wait(pool, e_ps, n)
                pool.tensor_tensor(
                    r_hl[:, :, :, :].rearrange("p s h q -> p (s h) q"),
                    tri[:, :].rearrange("p (a q) -> p a q", a=1).to_broadcast([P, 2 * H, P]),
                    a_hl[:, half, c, :, :].bitcast(F32).rearrange("p s (h a) -> p (s h) a", a=1)
                        .to_broadcast([P, 2 * H, P]),
                    ALU.mult).then_inc(r_rdy, 1)

            def decays(n):
                half, c = divmod(n, CPH)
                pool.wait_ge(dec_exp, n + 1)
                pool.affine_select(out=decay[:, :, :], in_=decay[:, :, :], compare_op=ALU.is_ge, fill=0.0,
                                   base=0, pattern=[[0, H], [1, P]], channel_multiplier=-1)\
                    .then_inc(dec_mask, 1)
                pool.wait_ge(dec_mask, n + 1)
                pool.wait_ge(soft, SOFT_STEPS * (half + 1))
                dt = dt_c[:, half, c, :]
                wait(pool, xs_rdy, n)
                pool.tensor_tensor(to_end[:, :], decay[:, :, P - 1], dt, ALU.mult).then_inc(end_rdy, 1)
                pool.wait_ge(end_rdy, n + 1)
                pool.tensor_tensor(decay[:, :, :], decay[:, :, :],
                                   dt.rearrange("p (h a) -> p h a", a=1).to_broadcast([P, H, P]),
                                   ALU.mult).then_inc(dec_dt, 1)
                pool.wait_ge(car_exp, n + 1)
                wait(pool, y_ps, n)
                pool.tensor_tensor(ce[:, :, :], carry[:, :, :],
                                   xbc[:, half, 2:CONV, c * P:(c + 1) * P], ALU.mult).then_inc(ce_rdy, 1)
                pool.wait_ge(att_mul, n + 1)
                pool.tensor_tensor(att[:, :, :], att[:, :, :], dskip_diag[:, :, :], ALU.add)\
                    .then_inc(att_d, 1)

            tri_times_a(0)
            decays(0)
            tri_times_a(1)
            for it in range(NCH + 1):
                if it + 1 < NCH:
                    decays(it + 1)
                if it + 2 < NCH:
                    tri_times_a(it + 2)
                if 1 <= it:
                    rms_of(1, NCH + it - 1, hsq, it)
                    pool.wait_ge(hid_rdy, it)
                    pool.tensor_tensor(resid[:, it - 1, :], resid[:, it - 1, :], hid[:, :], ALU.add)\
                        .then_inc(hx_rdy, 1)

            for s in range(len(STAGES)):
                for t in range(CPH):
                    n = s * CPH + t
                    pool.wait_ge(mv_rdy, n + 1)
                    pool.tensor_scalar(rstd[:, t:t + 1], mv[:, t, 1:2], EPS, None, ALU.add)\
                        .then_inc(ve_rdy, 1)
                    pool.wait_ge(ve_rdy, n + 1)
                    pool.tensor_tensor(rstd[:, t:t + 1], rstd[:, t:t + 1], half_neg[:, :], ALU.pow)\
                        .then_inc(rstd_rdy, 1)

        @block.tensor
        def _(pe):
            def three(dst, w_hi, w_lo, m_hi, m_lo, start, stop):
                pe.matmul(dst, w_hi, m_hi, start=start, stop=False)
                pe.matmul(dst, w_hi, m_lo, start=False, stop=False)
                return pe.matmul(dst, w_lo, m_hi, start=False, stop=stop)

            def transpose_chunk(dst, src, signal):
                for k in range(KT):
                    last = pe.transpose(dst[:, k * P:(k + 1) * P], src[:, k * P:(k + 1) * P], ident[:, :])
                last.then_inc(signal, 1)

            def x_t(c):
                pe.wait_ge(xn_rdy, c + 1)
                wait(pe, xt_lo, c - 1)
                transpose_chunk([B_E, B_O][c % 2], normed[:, c % 2, :], xt_ps)

            def project_pair(half, p):
                u = half * IN_PAIRS + p
                pe.wait_ge(plo, u + 1)
                for j in range(2):
                    if IN_TILES[2 * p + j][0] == "pad":
                        continue
                    n = half * IN_COUNT + 2 * p + j
                    wait(pe, in_free, n - 1)
                    for k in range(KT):
                        last = three(B_IN[n % 2][:, :], pair_hi[:, u % 2, j, k, :], pair_lo[:, u % 2, j, k, :],
                                     act_hi[:, half, k, :], act_lo[:, half, k, :], k == 0, k == KT - 1)
                    last.then_inc(in_ps, 1)

            def dt_t(half):
                pe.wait_ge(in_free, half * IN_COUNT + 1)
                wait(pe, dec_exp, 2 * half)
                for c in range(CPH):
                    last = pe.transpose(B_D[:, c * P:(c + 1) * P], dt_row[:, c * P:(c + 1) * P], ident[:, :])
                last.then_inc(dtt_ps, 1)

            def bx_t(n):
                half, c = divmod(n, CPH)
                pe.wait_ge(conv_rdy, half * CONV + 2)
                if n == 0:
                    pe.wait_ge(xt_lo, NCH)
                wait(pe, hid_rdy, n - 2)
                if n in (1, 2):
                    pe.wait_ge(bx_lo, n)
                    pe.wait_ge(xtok_rdy, n)
                for i, tile in enumerate((1, 0)):
                    last = pe.transpose(B_O[:, i * P:(i + 1) * P], xbc[:, half, tile, c * P:(c + 1) * P],
                                        ident[:, :])
                last.then_inc(bxt_ps, 1)

            def flat(t):
                return t.rearrange("p h q -> p (h q)")

            def scores(n):
                pe.wait_ge(cb_lo, n + 1)
                wait(pe, att_mul, n)
                three(B_S[:, :], b_hl[:, 0, :], b_hl[:, 1, :], flat(c_hl[:, 0, :, :]),
                      flat(c_hl[:, 1, :, :]), True, True).then_inc(s_ps, 1)
                pe.wait_ge(r_rdy, n + 1)
                wait(pe, dec_exp, n)
                if n == 0:
                    pe.wait_ge(soft, 1)
                    pe.wait_ge(ones_rdy, 2)
                if n == 2:
                    pe.wait_ge(soft, SOFT_STEPS + 1)
                for i in range(2):
                    last = pe.matmul(B_D[:, :], strict[:, :], flat(r_hl[:, i, :, :]), start=i == 0, stop=i == 1)
                last.then_inc(d_ps, 1)
                wait(pe, car_exp, n)
                wait(pe, h2t_lo, n - 3)
                for i in range(2):
                    last = pe.matmul(B_E[:, :], ones[:, :], flat(r_hl[:, i, :, :]), start=i == 0, stop=i == 1)
                last.then_inc(e_ps, 1)

            def mix(n):
                pe.wait_ge(ce_rdy, n + 1)
                wait(pe, st_rdy, n)
                wait(pe, y_rdy, n)
                if n == 0:
                    pe.wait_ge(zeroed, 6)
                for h in range(H):
                    pe.matmul(B_Y[:, h * P:(h + 1) * P], state[:, h, :], ce[:, h, :],
                              start=h == 0, stop=False, skip_group_check=True)
                pe.wait_ge(att_lo_s, n + 1)
                pe.wait_ge(bx_lo, n + 1)
                xh, xl = bx_hl[:, 0, 1, :], bx_hl[:, 1, 1, :]
                ah, al = flat(att_hl[:, 0, :, :]), flat(att_hl[:, 1, :, :])
                pe.matmul(B_Y[:, :], xh, ah, start=False, stop=False, skip_group_check=True)
                pe.matmul(B_Y[:, :], xh, al, start=False, stop=False, skip_group_check=True)
                pe.matmul(B_Y[:, :], xl, ah, start=False, stop=True, skip_group_check=True).then_inc(y_ps, 1)
                if n < NCH - 1:
                    pe.wait_ge(xs_lo_s, n + 1)
                    three(B_ST[:, :], bx_hl[:, 0, 0, :], bx_hl[:, 1, 0, :], flat(xs_hl[:, 0, :, :]),
                          flat(xs_hl[:, 1, :, :]), True, True).then_inc(st_ps, 1)

            def out_proj(n):
                if n == 0:
                    pe.wait_ge(dlo, H)
                pe.wait_ge(y_lo_s, n + 1)
                pe.wait_ge(bx_lo, min(n + 3, NCH))
                pe.wait_ge(xtok_rdy, min(n + 3, NCH))
                wait(pe, hid_rdy, n)
                for h in range(H):
                    last = three(B_O[:, :], y_hl[:, 0, h, :], y_hl[:, 1, h, :], wo_hi[:, h, :], wo_lo[:, h, :],
                                 h == 0, h == H - 1)
                last.then_inc(o_ps, 1)

            def h2_t(n):
                pe.wait_ge(h2_rdy, n + 1)
                pe.wait_ge(car_exp, min(n + 4, NCH))
                wait(pe, h2t_lo, n)
                transpose_chunk(B_E, normed[:, n % 2, :], h2t_ps)

            pe.wait_ge(masks, 3)
            for c in range(CPH):
                x_t(c)
            pe.wait_ge(xt_lo, CPH)
            for p in range(IN_PAIRS):
                project_pair(0, p)
                if p == 1:
                    dt_t(0)
                if p >= 2:
                    x_t(CPH + p - 2)
            bx_t(0)
            scores(0)
            for it in range(NCH + 2):
                if it + 1 < NCH:
                    scores(it + 1)
                if it < NCH:
                    mix(it)
                if it + 1 < NCH:
                    bx_t(it + 1)
                if it == 0:
                    pe.wait_ge(xt_lo, NCH)
                if 2 * it < IN_PAIRS:
                    project_pair(1, 2 * it)
                    project_pair(1, 2 * it + 1)
                    if it == 0:
                        dt_t(1)
                if 0 <= it - 2 < NCH:
                    h2_t(it - 2)
                if 0 <= it - 1 < NCH:
                    out_proj(it - 1)

            def gate_up(i, c, half):
                pe.wait_ge(plo, i * 2 + (c + U0 + 1))
                for j, (freed, signal) in enumerate(((silu_rdy, gate_ps), (g_rdy, up_ps))):
                    if c == 0:
                        pe.wait_ge(in_free, NHALF * IN_COUNT)
                    else:
                        pe.wait_ge(freed, i * 2 + c)
                    for k in range(KT):
                        last = three(B_IN[j][:, :], pair_hi[:, c % 2, j, k, :], pair_lo[:, c % 2, j, k, :],
                                     act_hi[:, half, k, :], act_lo[:, half, k, :], k == 0, k == KT - 1)
                    last.then_inc(signal, 1)

            def down(i, c, start, stop):
                pe.wait_ge(dlo, i * 2 + (c + H + 1))
                pe.wait_ge(g_lo_s, i * 2 + (c + 1))
                for t in range(CPH):
                    tok = slice(t * P, (t + 1) * P)
                    last = three(B_ACC[t][:, :], g_hl[c % 2][:, 0, tok], g_hl[c % 2][:, 1, tok],
                                 down_hi[:, c % 2, :], down_lo[:, c % 2, :], start, stop)
                last.then_inc(down_used, 1)

            def ln_t(half):
                for t in range(CPH):
                    n = half * CPH + t
                    pe.wait_ge(ln_rdy, n + 1)
                    wait(pe, lt_lo, n - 1)
                    transpose_chunk(B_NT[n % 2], resid[:, n, :], lt_ps)

            pe.wait_ge(h2t_lo, CPH)
            gate_up(0, 0, 0)
            for s, (p0, d0, n, half) in enumerate(STAGES):
                b = BASE[s]
                before, after = looped_pairs(s)
                gate_up(0, b + 1, half)
                if s:
                    pe.wait_ge(acc_free, CPH * s)
                else:
                    pe.wait_ge(h2t_lo, NCH)
                down(0, b, True, False)
                with pe.Fori(0, before) as i:
                    for j in range(2):
                        gate_up(i, b + 2 + j, half)
                        down(i, b + 1 + j, False, False)
                if s in (1, 2):
                    ln_t(s - 1)
                with pe.Fori(before, before + after) as i:
                    for j in range(2):
                        gate_up(i, b + 2 + j, half)
                        down(i, b + 1 + j, False, False)
                for k in range(2 * (before + after) + 2, n):
                    gate_up(0, b + k, half)
                    down(0, b + k - 1, False, False)
                if s + 1 < len(STAGES):
                    if s:
                        pe.wait_ge(lt_lo, CPH * s)
                    else:
                        pe.wait_ge(h2t_lo, NCH)
                    gate_up(0, b + n, STAGES[s + 1][3])
                down(0, b + n - 1, False, True)

        @block.scalar
        def _(act):
            def split_pair(i, c):
                act.wait_ge(pair_in[c % 2], i * 16 + 16 * (c // 2 + 1))
                act.activation(pair_hi[:, c % 2, :, :, :].rearrange("p j k f -> p (j k f)"),
                               pair_raw[:, c % 2, :, :, :].rearrange("p j k f -> p (j k f)"), ACT.Copy)\
                    .then_inc(phi, 1)

            def split_down(i, c, dst):
                act.wait_ge(down_in[c % 2], i * 16 + 16 * (c // 2 + 1))
                act.activation(dst, down_raw[:, c % 2, :], ACT.Copy).then_inc(dhi, 1)

            def square(src, which, c, signal):
                wait(act, xsq, NCH * which)
                wait(act, signal, c)
                act.activation(junk[:, :], src, ACT.Square, accum_out=ssq[:, which, c:c + 1])\
                    .then_inc(signal, 1)

            def transposed_hi(ps, count, b, n, signal):
                half, c = divmod(n, CPH)
                act.wait_ge(ps, count)
                act.activation(act_hi[:, half, :, c * P:(c + 1) * P], heads(b), ACT.Copy).then_inc(signal, 1)

            def conv_silu(half, m):
                j = CONV_ORDER[m]
                act.wait_ge(tap_dve, HALO * (half * CONV + m + 1))
                act.activation(xbc[:, half, j, :], xbc[:, half, j, :], ACT.Silu).then_inc(conv_rdy, 1)

            def leave(half, i):
                n = half * IN_COUNT + i
                kind, j = IN_TILES[i]
                act.wait_ge(in_ps, n + 1)
                b = B_IN[n % 2]
                if kind == "dt":
                    wait(act, dtt_ps, half)
                    act.activation(dt_row[:, :], b[:, :], ACT.Copy).then_inc(in_free, 1)
                elif kind == "conv":
                    if half:
                        act.wait_ge(tap_dve, HALO * i)
                        act.activation(cin[:, j, 0:HALO], cin[:, j, HT:HT + HALO], ACT.Copy)\
                            .then_inc(halo_rdy, 1)
                        act.wait_ge(halo_rdy, i)
                    act.activation(cin[:, j, HALO:HALO + HT], b[:, :], ACT.Copy).then_inc(cin_rdy, 1)
                    act.activation(xbc[:, half, j, :], b[:, :], ACT.Identity,
                                   scale=cw[:, j, HALO:TAPS], bias=cb[:, j:j + 1]).then_inc(in_free, 1)
                else:
                    act.activation(zs[:, half, j, :], b[:, :], ACT.Silu).then_inc(in_free, 1)

            def leave_pair(half, p):
                for i in (2 * p, 2 * p + 1):
                    if i < IN_COUNT:
                        leave(half, i)
                split_pair(0, half * IN_PAIRS + p + 2)

            def dt_exps(half):
                act.wait_ge(soft, SOFT_STEPS * half + 2)
                act.activation(dv[:, 1, :, :], dv[:, 1, :, :], ACT.Exp).then_inc(dt_exp, 1)

            def exps(n):
                act.wait_ge(d_ps, n + 1)
                wait(act, att_mul, n)
                act.activation(decay[:, :, :], heads(B_D), ACT.Exp).then_inc(dec_exp, 1)
                act.wait_ge(e_ps, n + 1)
                wait(act, ce_rdy, n)
                act.activation(carry[:, :, :], heads(B_E), ACT.Exp).then_inc(car_pre, 1)
                act.wait_ge(car_pre, n + 1)
                wait(act, st_rdy, n - 1)
                act.activation(carry_last[:, n % 2, :], carry[:, :, P - 1], ACT.Copy).then_inc(car_exp, 1)

            def cb_split(n):
                half, c = divmod(n, CPH)
                tok = slice(c * P, (c + 1) * P)
                act.wait_ge(conv_rdy, (half + 1) * CONV)
                wait(act, s_ps, n)
                act.activation(b_hl[:, 0, :], xbc[:, half, 1, tok], ACT.Copy).then_inc(cb_hi, 1)
                act.activation(c_hl[:, 0, :, :], xbc[:, half, 2:CONV, tok], ACT.Copy).then_inc(cb_hi, 1)

            def bx_split(n):
                act.wait_ge(bxt_ps, n + 1)
                wait(act, st_ps, n)
                act.activation(bx_hl[:, 0, :, :], B_O[:, 0:2 * P].rearrange("p (i q) -> p i q", i=2), ACT.Copy)\
                    .then_inc(bx_hi, 1)
                wait(act, xs_rdy, n)
                act.activation(x_tok[:, :], B_O[:, P:2 * P], ACT.Copy).then_inc(xtok_rdy, 1)

            def att_split(n):
                act.wait_ge(att_d, n + 1)
                wait(act, y_ps, n)
                act.activation(att_hl[:, 0, :, :], att[:, :, :], ACT.Copy).then_inc(att_hi_s, 1)

            def xs_split(n):
                act.wait_ge(xs_rdy, n + 1)
                wait(act, st_ps, n)
                act.activation(xs_hl[:, 0, :, :], xs[:, :, :], ACT.Copy).then_inc(xs_hi_s, 1)

            def y_split(n):
                act.wait_ge(y_rdy, n + 1)
                wait(act, o_ps, n)
                act.activation(y_hl[:, 0, :, :], y[:, :, :], ACT.Copy).then_inc(y_hi_s, 1)

            for c in range(CPH):
                act.wait_ge(x_in[c], 16)
                square(resid[:, c, :], 0, c, xsq)
                if c < 2:
                    split_pair(0, c)
            for c in range(CPH):
                transposed_hi(xt_ps, c + 1, [B_E, B_O][c % 2], c, xt_hi)
            act.wait_ge(consts_in, CONSTS * 16)
            act.activation(neg_a[:, :], neg_a[:, :], ACT.Exp).then_inc(aexp_rdy, 1)
            for c in range(CPH, NCH):
                act.wait_ge(x_in[c], 16)
                square(resid[:, c, :], 0, c, xsq)
            for p in range(IN_PAIRS):
                leave_pair(0, p)
                if p == 1:
                    dt_exps(0)
                if p == 3:
                    for m in range(CONV):
                        conv_silu(0, m)
                if p == 3 or p == 5:
                    for v in (p - 3, p - 2):
                        split_down(0, v, wo_hi[:, v, :])
                if p >= 2:
                    transposed_hi(xt_ps, CPH + p - 1, [B_E, B_O][p % 2], CPH + p - 2, xt_hi)
            cb_split(0)
            bx_split(0)
            exps(0)
            cb_split(1)
            att_split(0)
            xs_split(0)
            for it in range(NCH + 2):
                if it + 1 < NCH:
                    exps(it + 1)
                if it + 1 < NCH:
                    bx_split(it + 1)
                    att_split(it + 1)
                    if it + 1 < NCH - 1:
                        xs_split(it + 1)
                if 2 * it < IN_PAIRS:
                    leave_pair(1, 2 * it)
                    leave_pair(1, 2 * it + 1)
                    if it == 0:
                        dt_exps(1)
                    for m in range(3 * it, min(3 * it + 3, CONV)):
                        conv_silu(1, m)
                if it + 2 < NCH:
                    cb_split(it + 2)
                if 0 <= it - 2 < NCH:
                    transposed_hi(h2t_ps, it - 1, B_E, it - 2, h2t_hi)
                if it < NCH:
                    y_split(it)
                if 0 <= it - 1 < NCH:
                    act.wait_ge(hid_rdy, it)
                    square(hid[:, :], 1, it - 1, hsq)
            split_down(0, H, down_hi[:, 0, :])

            def gated_step(i, c):
                act.wait_ge(gate_ps, i * 2 + (c + 1))
                if c:
                    act.wait_ge(g_rdy, i * 2 + c)
                act.activation(gate_s, B_IN[0][:, :], ACT.Silu).then_inc(silu_rdy, 1)
                if c < STEPS - 2:
                    act.wait_ge(up_ps, i * 2 + (c + 1))
                    split_pair(i, c + U0 + 2)
                act.wait_ge(g_rdy, i * 2 + (c + 1))
                act.activation(g_hl[c % 2][:, 0, :], gated, ACT.Copy).then_inc(g_hi_s, 1)
                if c < STEPS - 1:
                    if c:
                        act.wait_ge(down_used, i * 2 + c)
                    split_down(i, c + H + 1, down_hi[:, (c + 1) % 2, :])

            def ln_hi(half):
                for t in range(CPH):
                    n = half * CPH + t
                    transposed_hi(lt_ps, n + 1, B_NT[n % 2], n, lt_hi)

            for s, (p0, d0, n, half) in enumerate(STAGES):
                b = BASE[s]
                before, after = looped_pairs(s)
                gated_step(0, b)
                gated_step(0, b + 1)
                with act.Fori(0, before) as i:
                    for j in range(2):
                        gated_step(i, b + 2 + j)
                if s in (1, 2):
                    ln_hi(s - 1)
                with act.Fori(before, before + after) as i:
                    for j in range(2):
                        gated_step(i, b + 2 + j)
                for k in range(2 * (before + after) + 2, n):
                    gated_step(0, b + k)

        @block.vector
        def _(dve):
            def f32(t):
                return t.bitcast(F32)

            def pair_rest(i, c):
                dve.wait_ge(phi, i * 2 + (c + 1))
                dve.tensor_tensor(pair_lo[:, c % 2, :, :, :].rearrange("p j k f -> p (j k f)"),
                                  pair_raw[:, c % 2, :, :, :].rearrange("p j k f -> p (j k f)"),
                                  f32(pair_hi[:, c % 2, :, :, :].rearrange("p j k f -> p (j k f)")),
                                  ALU.subtract).then_inc(plo, 1)

            def down_rest(i, c, hi, lo):
                dve.wait_ge(dhi, i * 2 + (c + 1))
                dve.tensor_tensor(lo, down_raw[:, c % 2, :], f32(hi), ALU.subtract).then_inc(dlo, 1)

            def x_norm(c):
                dve.wait_ge(rms_rdy, c + 1)
                wait(dve, xt_ps, c - 1)
                dve.scalar_tensor_tensor(out=normed[:, c % 2, :], in0=resid[:, c, :], scalar=rms[:, 0, c:c + 1],
                                         in1=ln_b[:, :], op0=ALU.mult, op1=ALU.mult).then_inc(xn_rdy, 1)

            def transposed_lo(hi_signal, count, b, n, signal):
                half, c = divmod(n, CPH)
                tok = slice(c * P, (c + 1) * P)
                dve.wait_ge(hi_signal, count)
                dve.tensor_tensor(act_lo[:, half, :, tok], heads(b), f32(act_hi[:, half, :, tok]), ALU.subtract)\
                    .then_inc(signal, 1)

            def taps(half, m):
                j = CONV_ORDER[m]
                dve.wait_ge(in_free, half * IN_COUNT + m + 2)
                if half == 0 and m == 0:
                    dve.wait_ge(zeroed, 6)
                for k in range(HALO):
                    wait(dve, tap_dve, HALO * (half * CONV + m) + k)
                    dve.scalar_tensor_tensor(out=xbc[:, half, j, :], in0=cin[:, j, k:k + HT],
                                             scalar=cw[:, j, k:k + 1], in1=xbc[:, half, j, :],
                                             op0=ALU.mult, op1=ALU.add).then_inc(tap_dve, 1)

            def per_head(t):
                return t.rearrange("p (a h) -> p a h", a=1).to_broadcast([P, CPH, H])

            def softplus(half):
                done = [SOFT_STEPS * half]

                def step(instruction):
                    instruction.then_inc(soft, 1)
                    done[0] += 1
                    dve.wait_ge(soft, done[0])

                v, e, t, p = (dv[:, i, :, :] for i in range(4))
                dt, a = dt_c[:, half, :, :], a_c[:, :, :]
                dve.wait_ge(dtt_ps, half + 1)
                step(dve.tensor_tensor(v, heads(B_D)[:, :, 0:H], per_head(dtb_b[:, :]), ALU.add))
                step(dve.scalar_tensor_tensor(out=e, in0=v, scalar=-1.0, in1=v, op0=ALU.mult, op1=ALU.min))
                dve.wait_ge(dt_exp, half + 1)
                step(dve.tensor_scalar(t, e, 2.0, None, ALU.add))
                step(dve.reciprocal(t, t))
                step(dve.tensor_tensor(e, e, t, ALU.mult))
                step(dve.tensor_tensor(t, e, e, ALU.mult))
                step(dve.tensor_scalar(p, t, ATANH[-1], None, ALU.mult))
                for c in ATANH[-2:0:-1]:
                    step(dve.scalar_tensor_tensor(out=p, in0=p, scalar=c, in1=t, op0=ALU.add, op1=ALU.mult))
                step(dve.scalar_tensor_tensor(out=p, in0=p, scalar=ATANH[0], in1=e, op0=ALU.add, op1=ALU.mult))
                step(dve.tensor_scalar(v, v, 0.0, None, ALU.max))
                step(dve.scalar_tensor_tensor(out=dt, in0=p, scalar=2.0, in1=v, op0=ALU.mult, op1=ALU.add))
                step(dve.tensor_tensor(a, dt, per_head(neg_a[:, :]), ALU.mult))
                step(dve.tensor_copy(a_hl[:, half, :, 0, :], a))
                step(dve.tensor_tensor(a_hl[:, half, :, 1, :], a, f32(a_hl[:, half, :, 0, :]), ALU.subtract))
                assert done[0] == SOFT_STEPS * (half + 1)

            def cb_rest(n):
                half, c = divmod(n, CPH)
                tok = slice(c * P, (c + 1) * P)
                dve.wait_ge(cb_hi, 2 * (n + 1))
                dve.tensor_tensor(b_hl[:, 1, :], xbc[:, half, 1, tok], f32(b_hl[:, 0, :]), ALU.subtract)\
                    .then_inc(b_lo, 1)
                dve.tensor_tensor(c_hl[:, 1, :, :], xbc[:, half, 2:CONV, tok], f32(c_hl[:, 0, :, :]), ALU.subtract)\
                    .then_inc(cb_lo, 1)

            def bx_rest(n):
                dve.wait_ge(xtok_rdy, n + 1)
                dve.tensor_tensor(bx_hl[:, 1, :, :], B_O[:, 0:2 * P].rearrange("p (i q) -> p i q", i=2),
                                  f32(bx_hl[:, 0, :, :]), ALU.subtract).then_inc(bx_lo, 1)

            def att_product(n):
                dve.wait_ge(s_ps, n + 1)
                dve.wait_ge(dec_dt, n + 1)
                wait(dve, att_lo_s, n)
                dve.tensor_tensor(att[:, :, :], heads(B_S), decay[:, :, :], ALU.mult).then_inc(att_mul, 1)

            def att_rest(n):
                dve.wait_ge(att_hi_s, n + 1)
                dve.tensor_tensor(att_hl[:, 1, :, :], att[:, :, :], f32(att_hl[:, 0, :, :]), ALU.subtract)\
                    .then_inc(att_lo_s, 1)

            def xs_product(n):
                dve.wait_ge(xtok_rdy, n + 1)
                dve.wait_ge(end_rdy, n + 1)
                wait(dve, xs_lo_s, n)
                dve.tensor_tensor(xs[:, :, :],
                                  x_tok[:, :].rearrange("p (a q) -> p a q", a=1).to_broadcast([P, H, P]),
                                  to_end[:, :].rearrange("p (h a) -> p h a", a=1).to_broadcast([P, H, P]),
                                  ALU.mult).then_inc(xs_rdy, 1)

            def xs_rest(n):
                dve.wait_ge(xs_hi_s, n + 1)
                dve.tensor_tensor(xs_hl[:, 1, :, :], xs[:, :, :], f32(xs_hl[:, 0, :, :]), ALU.subtract)\
                    .then_inc(xs_lo_s, 1)

            def y_gate(n):
                half, c = divmod(n, CPH)
                dve.wait_ge(in_free, (half + 1) * IN_COUNT)
                dve.wait_ge(y_ps, n + 1)
                wait(dve, y_lo_s, n)
                dve.tensor_tensor(y[:, :, :], heads(B_Y), zs[:, half, :, c * P:(c + 1) * P], ALU.mult)\
                    .then_inc(y_rdy, 1)

            def y_rest(n):
                dve.wait_ge(y_hi_s, n + 1)
                dve.tensor_tensor(y_hl[:, 1, :, :], y[:, :, :], f32(y_hl[:, 0, :, :]), ALU.subtract)\
                    .then_inc(y_lo_s, 1)

            def update_state(n):
                dve.wait_ge(st_ps, n + 1)
                dve.wait_ge(car_exp, n + 1)
                wait(dve, st_rdy, n)
                for h in range(H):
                    last = dve.scalar_tensor_tensor(out=state[:, h, :], in0=state[:, h, :],
                                                    scalar=carry_last[:, n % 2, h:h + 1],
                                                    in1=B_ST[:, h * P:(h + 1) * P], op0=ALU.mult, op1=ALU.add)
                last.then_inc(st_rdy, 1)

            def hidden(n):
                dve.wait_ge(o_ps, n + 1)
                wait(dve, hx_rdy, n)
                wait(dve, hsq, n)
                wait(dve, h2_rdy, n)
                dve.tensor_tensor(hid[:, :], B_O[:, :], resid[:, n, :], ALU.add).then_inc(hid_rdy, 1)

            def h2_norm(n):
                dve.wait_ge(rms_rdy, NCH + n + 1)
                dve.wait_ge(ln2_in, 16)
                wait(dve, h2t_ps, n - 1)
                if n < 2:
                    dve.wait_ge(xt_ps, NCH)
                dve.scalar_tensor_tensor(out=normed[:, n % 2, :], in0=hid[:, :], scalar=rms[:, 1, n:n + 1],
                                         in1=ln_b[:, :], op0=ALU.mult, op1=ALU.mult).then_inc(h2_rdy, 1)

            dve.wait_ge(masks, 3)
            dve.tensor_copy(strict[:, :], strict_f[:, :]).then_inc(ones_rdy, 1)
            dve.tensor_scalar(ones[:, :], strict_f[:, :], 0.0, 1.0, ALU.mult, ALU.add).then_inc(ones_rdy, 1)
            dve.wait_ge(consts_in, CONSTS * 16)
            x_norm(0)
            x_norm(1)
            pair_rest(0, 0)
            for c in range(CPH):
                transposed_lo(xt_hi, c + 1, [B_E, B_O][c % 2], c, xt_lo)
                if c + 2 < CPH:
                    x_norm(c + 2)
                if c == 1:
                    pair_rest(0, 1)
            dve.wait_ge(aexp_rdy, 1)
            dve.tensor_scalar(neg_a[:, :], neg_a[:, :], -1.0, None, ALU.mult).then_inc(nega_rdy, 1)
            dve.wait_ge(nega_rdy, 1)
            for p in range(IN_PAIRS):
                for m in (2 * p - 1, 2 * p):
                    if 0 <= m < CONV:
                        taps(0, m)
                pair_rest(0, p + 2)
                if p == 1:
                    softplus(0)
                    x_norm(CPH)
                    x_norm(CPH + 1)
                if p == 3 or p == 5:
                    for v in (p - 3, p - 2):
                        down_rest(0, v, wo_hi[:, v, :], wo_lo[:, v, :])
                if p >= 2:
                    transposed_lo(xt_hi, CPH + p - 1, [B_E, B_O][p % 2], CPH + p - 2, xt_lo)
                if 2 <= p < 4:
                    x_norm(CPH + p)
            cb_rest(0)
            bx_rest(0)
            cb_rest(1)
            att_product(0)
            xs_product(0)
            att_rest(0)
            xs_rest(0)
            for it in range(NCH + 2):
                if it + 1 < NCH:
                    att_product(it + 1)
                if it < NCH:
                    y_gate(it)
                if it + 1 < NCH:
                    bx_rest(it + 1)
                    update_state(it)
                    att_rest(it + 1)
                    if it + 1 < NCH - 1:
                        xs_product(it + 1)
                        xs_rest(it + 1)
                if 2 * it < IN_PAIRS:
                    for p in (2 * it, 2 * it + 1):
                        for m in (2 * p - 1, 2 * p):
                            if 0 <= m < CONV:
                                taps(1, m)
                        pair_rest(0, IN_PAIRS + p + 2)
                    if it == 0:
                        softplus(1)
                if it + 2 < NCH:
                    cb_rest(it + 2)
                if 0 <= it - 2 < NCH:
                    transposed_lo(h2t_hi, it - 1, B_E, it - 2, h2t_lo)
                if 0 <= it - 1 < NCH:
                    hidden(it - 1)
                if it < NCH:
                    y_rest(it)
                if 0 <= it - 1 < NCH:
                    h2_norm(it - 1)
            down_rest(0, H, down_hi[:, 0, :], down_lo[:, 0, :])

            def gated_step(i, c):
                dve.wait_ge(silu_rdy, i * 2 + (c + 1))
                dve.wait_ge(up_ps, i * 2 + (c + 1))
                if c:
                    dve.wait_ge(g_lo_s, i * 2 + c)
                dve.tensor_tensor(gated, B_IN[1][:, :], gate_s, ALU.mult).then_inc(g_rdy, 1)
                if c < STEPS - 2:
                    pair_rest(i, c + U0 + 2)
                dve.wait_ge(g_hi_s, i * 2 + (c + 1))
                dve.tensor_tensor(g_hl[c % 2][:, 1, :], gated, f32(g_hl[c % 2][:, 0, :]), ALU.subtract)\
                    .then_inc(g_lo_s, 1)
                if c < STEPS - 1:
                    down_rest(i, c + H + 1, down_hi[:, (c + 1) % 2, :], down_lo[:, (c + 1) % 2, :])

            def ln_stats(s):
                base, half = s * CPH, STAGES[s][3]
                dve.wait_ge(down_used, BASE[s] + STAGES[s][2])
                dve.wait_ge(hx_rdy, NCH)
                for t in range(CPH):
                    n = half * CPH + t
                    dve.tensor_tensor(resid[:, n, :], B_ACC[t][:, :], resid[:, n, :], ALU.add)\
                        .then_inc(acc_free, 1)
                for t in range(CPH):
                    dve.wait_ge(acc_free, base + t + 1)
                    dve.bn_stats(bn[:, t, :], resid[:, half * CPH + t, :]).then_inc(bn_rdy, 1)
                for t in range(CPH):
                    dve.wait_ge(bn_rdy, base + t + 1)
                    dve.bn_aggr(mv[:, t, :], bn[:, t, :]).then_inc(mv_rdy, 1)

            def ln_apply(s):
                half = STAGES[s][3]
                for t in range(CPH):
                    n = half * CPH + t
                    dve.wait_ge(rstd_rdy, s * CPH + t + 1)
                    dve.tensor_scalar(resid[:, n, :], resid[:, n, :], mv[:, t, 0:1], rstd[:, t:t + 1],
                                      ALU.subtract, ALU.mult).then_inc(ln_rdy, 1)

            def ln_lo(half):
                for t in range(CPH):
                    n = half * CPH + t
                    transposed_lo(lt_hi, n + 1, B_NT[n % 2], n, lt_lo)

            for s, (p0, d0, n, half) in enumerate(STAGES):
                b = BASE[s]
                before, after = looped_pairs(s)
                gated_step(0, b)
                if s:
                    ln_stats(s - 1)
                gated_step(0, b + 1)
                if s:
                    ln_apply(s - 1)
                with dve.Fori(0, before) as i:
                    for j in range(2):
                        gated_step(i, b + 2 + j)
                if s in (1, 2):
                    ln_lo(s - 1)
                with dve.Fori(before, before + after) as i:
                    for j in range(2):
                        gated_step(i, b + 2 + j)
                for k in range(2 * (before + after) + 2, n):
                    gated_step(0, b + k)
            ln_stats(len(STAGES) - 1)
            ln_apply(len(STAGES) - 1)


def looped_pairs(s):
    pairs = (STAGES[s][2] - 2) // 2 - (s == len(STAGES) - 1)
    return pairs // 2, pairs - pairs // 2


def _feature_tiles(w, tiles):
    padded = np.zeros((tiles * P, DM), w.dtype)
    padded[:w.shape[0]] = w
    return padded.reshape(tiles, P, KT, P).transpose(0, 3, 2, 1)


def _down_tiles(w, tiles):
    padded = np.zeros((tiles * P, DM), w.dtype)
    padded[:w.shape[1]] = w.T
    return padded.reshape(tiles, P, DM)


def kernel(**inputs):
    import concourse.bacc as bacc
    from concourse.bass_utils import run_bass_kernel_spmd

    a = {k[3:]: np.asarray(v) for k, v in inputs.items()}
    w_in = _feature_tiles(a["attn_w_in"], 11)
    row = {"z": 0, "conv": H, "dt": 10}
    blank = np.zeros_like(w_in[0])
    firsts = [blank if kind == "pad" else w_in[row[kind] + j] for kind, j in IN_TILES]
    projections = np.stack(firsts).reshape(IN_PAIRS, 2, P, KT, P)
    mlp = np.stack([_feature_tiles(a[f"attn_{n}_w"], T_MLP) for n in ("gate", "up")], axis=1)
    ffn = np.stack([_feature_tiles(a[f"ffn_W_{n}"], T_FFN) for n in ("gate", "up")], axis=1)
    arrays = {
        "x": a["attn_hidden_states"].reshape(NCH, P, DM),
        "pairs": np.concatenate([projections, mlp, ffn]).transpose(0, 2, 1, 3, 4),
        "downs": np.concatenate([_down_tiles(a["attn_w_out"], H), _down_tiles(a["attn_down_w"], T_MLP),
                                 _down_tiles(a["ffn_W_down"], T_FFN)]),
        "conv_w": a["attn_conv_w"].reshape(CONV, P, TAPS).transpose(1, 0, 2),
        "conv_b": a["attn_conv_b"].reshape(CONV, P).T,
        "a_log": a["attn_A_log"].reshape(1, H),
        "d_skip": a["attn_D"].reshape(1, H),
        "dt_bias": a["attn_dt_bias"].reshape(1, H),
        "ln1": a["attn_ln1_w"].reshape(1, DM),
        "ln2": a["attn_ln2_w"].reshape(1, DM),
    }
    arrays = {f"in_{k}": np.ascontiguousarray(v) for k, v in arrays.items()}
    nc = bacc.Bacc("TRN2", target_bir_lowering=False, num_devices=1)
    args = [nc.dram_tensor(k, v.shape, F32, kind="ExternalInput").ap() for k, v in arrays.items()]
    out = nc.dram_tensor("out", (NCH, P, DM), F32, kind="ExternalOutput").ap()
    build(nc, *args, out)
    result = run_bass_kernel_spmd(nc, [arrays], core_ids=[0])
    return result.results[0]["out"].reshape(1, L, DM)
```

```python
from contextlib import ExitStack

import numpy as np

import concourse.bass as bass
from concourse import mybir

F32 = mybir.dt.float32
F32R = mybir.dt.float32r
ALU = mybir.AluOpType
ACT = mybir.ActivationFunctionType

P = 128
L = 1024
DM = 512
KT = DM // P
H = 4
NCH = L // P
NHALF = 2
CPH = NCH // NHALF
HT = L // NHALF
TAPS = 4
HALO = TAPS - 1
CONV = 6
EPS = 1e-5
NEVER = -1e30
F_MLP, F_FFN = 1792, 1376
T_MLP = F_MLP // P
T_FFN = -(-F_FFN // P)
IN_TILES = [("dt", 0), ("conv", 1), ("conv", 0), ("conv", 2), ("conv", 3), ("conv", 4),
            ("conv", 5), ("z", 0), ("z", 1), ("z", 2), ("z", 3), ("pad", 0)]
IN_PAIRS = len(IN_TILES) // 2
STAGES = [(IN_PAIRS, H, T_MLP, 0), (IN_PAIRS, H, T_MLP, 1),
          (IN_PAIRS + T_MLP, H + T_MLP, T_FFN, 0), (IN_PAIRS + T_MLP, H + T_MLP, T_FFN, 1)]
BASE = [0, T_MLP, 2 * T_MLP, 2 * T_MLP + T_FFN]
STEPS = 2 * (T_MLP + T_FFN)
U0 = NHALF * IN_PAIRS
CONSTS = 5
SOFT_STEPS = 24
BETWEEN = {(-1, 2): (0,), (0, 0): (1,), (0, 1): (2,), (0, 2): (3,), (1, 0): (4,), (1, 1): (5,), (1, 2): (6,),
           (2, 1): (7,), (2, 2): (8,), (3, 1): (9,), (3, 2): (10,)}
CONV_ORDER = [j for kind, j in IN_TILES if kind == "conv"]
IN_COUNT = len(IN_TILES) - 1
ATANH = [1.0 / (2 * n + 1) for n in range(8)]


def build(nc, x, pairs, downs, conv_w, conv_b, a_log, d_skip, dt_bias, ln1, ln2, out):
    ctx = ExitStack()
    with ctx:
        def sb(name, shape, dt=F32):
            return ctx.enter_context(nc.sbuf_tensor(name, shape, dt))

        def sem(name):
            return ctx.enter_context(nc.semaphore(name))

        resid = sb("resid", [P, NCH, DM])
        act_hi = sb("act_hi", [P, NHALF, KT, HT], F32R)
        act_lo = sb("act_lo", [P, NHALF, KT, HT], F32R)
        zs = sb("zs", [P, NHALF, H, HT])
        cin = sb("cin", [P, CONV, HALO + HT])
        xbc = sb("xbc", [P, NHALF, CONV, HT])
        wo_hi = sb("wo_hi", [P, H, DM], F32R)
        wo_lo = sb("wo_lo", [P, H, DM], F32R)
        pair_raw = sb("pair_raw", [P, 2, 2, KT, P])
        pair_hi = sb("pair_hi", [P, 2, 2, KT, P], F32R)
        pair_lo = sb("pair_lo", [P, 2, 2, KT, P], F32R)
        down_raw = sb("down_raw", [P, 2, DM])
        down_hi = sb("down_hi", [P, 2, DM], F32R)
        down_lo = sb("down_lo", [P, 2, DM], F32R)

        ident = sb("ident", [P, P])
        tri = sb("tri", [P, P])
        strict_f = sb("strict_f", [P, P])
        strict = sb("strict", [P, P], F32R)
        ident_r = sb("ident_r", [P, P], F32R)
        never_f = sb("never_f", [P, P])
        never = sb("never", [P, H, P], F32R)
        ones = sb("ones", [P, P], F32R)
        ln_b = sb("ln_b", [P, DM])
        dskip_b = sb("dskip_b", [P, H])
        dskip_diag = sb("dskip_diag", [P, H, P])
        dtb_b = sb("dtb_b", [P, H])
        neg_a = sb("neg_a", [P, H])
        cw = sb("cw", [P, CONV, TAPS])
        cb = sb("cb", [P, CONV])
        half_neg = sb("half_neg", [P, 1])
        minus_one = sb("minus_one", [P, 1])

        dt_row = sb("dt_row", [P, HT])
        dv = sb("dv", [P, 6, CPH, H])
        dt_c = sb("dt_c", [P, NHALF, CPH, H])
        a_c = sb("a_c", [P, CPH, H])
        a_hl = sb("a_hl", [P, NHALF, CPH, 2, H], F32R)

        bx = sb("bx", [P, 2, 2, P])
        r_hl = sb("r_hl", [P, 2, H, P], F32R)
        decay = sb("decay", [P, H, P])
        carry = sb("carry", [P, H, P])
        carry_last = sb("carry_last", [P, 2, H])
        ce = sb("ce", [P, H, P])
        att = sb("att", [P, 2, H, P])
        to_end = sb("to_end", [P, 2, H])
        xs = sb("xs", [P, 2, H, P])
        state = sb("state", [P, H, P])
        y = sb("y", [P, H, P])
        y_hl = sb("y_hl", [P, 2, 2, H, P], F32R)
        hid = sb("hid", [P, DM])
        normed = sb("normed", [P, 2, DM])
        junk = sb("junk", [P, DM], mybir.dt.bfloat16)
        ssq = sb("ssq", [P, 2, NCH])
        rms = sb("rms", [P, 2, NCH])
        bn = sb("bn", [P, CPH, 6])
        mv = sb("mv", [P, CPH, 2])
        rstd = sb("rstd", [P, CPH])
        gate_s = decay[:, :, :].rearrange("p h q -> p (h q)")
        gated = att[:, 0, :, :].rearrange("p h q -> p (h q)")
        g_hl = [r_hl[:, :, :, :].rearrange("p s h q -> p s (h q)"),
                y_hl[:, 0, :, :, :].rearrange("p s h q -> p s (h q)")]

        bank = [ctx.enter_context(nc.psum_tensor(f"bank{i}", [P, DM], F32)) for i in range(8)]
        B_IN = bank[0:2]
        B_S, B_D, B_E, B_Y, B_ST, B_O = bank[2:8]
        B_ACC = bank[2:6]
        B_BX = bank[1]
        B_NT = [bank[6], bank[7]]

        def in_bank(half, i):
            return B_IN[0 if half else i % 2]

        def h2_bank(n):
            return B_E if n < NCH - 2 else B_ST

        def heads(b):
            return b[:, :].rearrange("p (h q) -> p h q", h=H)

        consts_in, ln1_in, ln2_in = sem("consts_in"), sem("ln1_in"), sem("ln2_in")
        x_in = [sem(f"x_in{c}") for c in range(NCH)]
        pair_in = [sem(f"pair_in{i}") for i in range(2)]
        down_in = [sem(f"down_in{i}") for i in range(2)]
        zeroed, masks, ones_rdy, diag_rdy, nega_rdy, aexp_rdy = map(
            sem, ("zeroed", "masks", "ones_rdy", "diag_rdy", "nega_rdy", "aexp_rdy"))
        phi, plo, pair_used, dhi, dlo, down_used = map(
            sem, ("pair_hi_rdy", "pair_lo_rdy", "pair_used", "down_hi_rdy", "down_lo_rdy", "down_used"))
        xsq, hsq, ms_rdy, rms_rdy, xn_rdy, xt_ps, xt_hi, xt_lo = map(
            sem, ("xsq", "hsq", "ms_rdy", "rms_rdy", "xn_rdy", "xt_ps", "xt_hi", "xt_lo"))
        in_ps, in_free = sem("in_ps"), sem("in_free")
        cin_rdy, halo_rdy, tap_dve, conv_rdy, car_pre = map(
            sem, ("cin_rdy", "halo_rdy", "tap_dve", "conv_rdy", "car_pre"))
        dtt_ps, dt_sum, soft, dt_exp = map(sem, ("dtt_ps", "dt_sum", "soft", "dt_exp"))
        bxt_ps, bx_rdy = sem("bxt_ps"), sem("bx_rdy")
        r_rdy, s_ps, d_ps, e_ps, dec_exp, car_exp, end_rdy = map(
            sem, ("r_rdy", "s_ps", "d_ps", "e_ps", "dec_exp", "car_exp", "end_rdy"))
        att_mul, att_d, ce_rdy, xs_rdy = map(sem, ("att_mul", "att_d", "ce_rdy", "xs_rdy"))
        y_ps, st_ps, st_rdy, y_rdy, y_hi_s, y_lo_s = map(
            sem, ("y_ps", "st_ps", "state_rdy", "y_rdy", "y_hi_rdy", "y_lo_rdy"))
        o_ps, hid_rdy, hx_rdy, h2_rdy, h2t_ps, h2t_hi, h2t_lo = map(
            sem, ("o_ps", "hid_rdy", "hx_rdy", "h2_rdy", "h2t_ps", "h2t_hi", "h2t_lo"))
        up_ps, gate_ps, silu_rdy, g_rdy, g_hi_s, g_lo_s = map(
            sem, ("up_ps", "gate_ps", "silu_rdy", "g_rdy", "g_hi_rdy", "g_lo_rdy"))
        acc_ps, acc_free, bn_rdy, mv_rdy, ve_rdy, rstd_rdy, ln_rdy, lt_ps, lt_hi, lt_lo = map(
            sem, ("acc_ps", "acc_free", "bn_rdy", "mv_rdy", "ve_rdy", "rstd_rdy", "ln_rdy", "lt_ps", "lt_hi", "lt_lo"))
        out_done = sem("out_done")

        def per_head(t):
            return t.rearrange("p (a h) -> p a h", a=1).to_broadcast([P, CPH, H])

        def wait(eng, s, value):
            if not isinstance(value, int) or value > 0:
                eng.wait_ge(s, value)

        block = ctx.enter_context(nc.Block())

        @block.sync
        def _(sp):
            def load_pair(u, tile, slot):
                wait(sp, plo, u - 1)
                sp.dma_start(pair_raw[:, slot, :, :, :], pairs[tile]).then_inc(pair_in[slot], 16)

            def load_down(v, tile, slot):
                wait(sp, dlo, v - 1)
                sp.dma_start(down_raw[:, slot, :], downs[tile]).then_inc(down_in[slot], 16)

            for c in range(CPH):
                sp.dma_start(resid[:, c, :], x[c]).then_inc(x_in[c], 16)
                if c == 0:
                    sp.dma_start(ln_b[:, :], ln1.to_broadcast([P, DM])).then_inc(ln1_in, 16)
            load_pair(0, 0, 0)
            load_pair(1, 1, 1)
            for dst, src in ((cw[:, :, :], conv_w), (cb[:, :], conv_b),
                             (dtb_b[:, :], dt_bias.to_broadcast([P, H])),
                             (neg_a[:, :], a_log.to_broadcast([P, H])),
                             (dskip_b[:, :], d_skip.to_broadcast([P, H]))):
                sp.dma_start(dst, src).then_inc(consts_in, 16)
            for c in range(CPH, NCH):
                sp.dma_start(resid[:, c, :], x[c]).then_inc(x_in[c], 16)
            load_down(0, 0, 0)
            load_down(1, 1, 1)
            for u in range(2, U0 + 2):
                load_pair(u, u % IN_PAIRS if u < U0 else IN_PAIRS + u - U0, u % 2)
                if u == 9:
                    sp.wait_ge(xn_rdy, NCH)
                    sp.dma_start(ln_b[:, :], ln2.to_broadcast([P, DM])).then_inc(ln2_in, 16)
                if u == 6:
                    load_down(2, 2, 0)
                    load_down(3, 3, 1)
            load_down(H, H, 0)

            for s, (p0, d0, n, half) in enumerate(STAGES):
                b = BASE[s]
                looped = (n - 2) // 2
                with sp.Fori(0, looped) as i:
                    for j in range(2):
                        load_pair(i * 2 + (U0 + b + j + 2), i * 2 + (p0 + j + 2), (b + j) % 2)
                        load_down(i * 2 + (H + b + j + 1), i * 2 + (d0 + j + 1), (b + j + 1) % 2)
                for k in range(2 * looped, n):
                    g = b + k
                    following = STAGES[s + 1] if s + 1 < len(STAGES) else None
                    if k + 2 < n:
                        load_pair(U0 + g + 2, p0 + k + 2, g % 2)
                    elif following:
                        load_pair(U0 + g + 2, following[0] + k + 2 - n, g % 2)
                    if k + 1 < n:
                        load_down(H + g + 1, d0 + k + 1, (g + 1) % 2)
                    elif following:
                        load_down(H + g + 1, following[1], (g + 1) % 2)
            for half in range(NHALF):
                for t in range(CPH):
                    wait(sp, ln_rdy, (NHALF + half) * CPH + t + 1)
                    sp.dma_start(out[half * CPH + t], resid[:, half * CPH + t, :]).then_inc(out_done, 16)
            sp.wait_ge(out_done, 16 * NCH)

        @block.gpsimd
        def _(pool):
            pool.memset(ident[:, :], 0.0).then_inc(zeroed, 1)
            pool.memset(half_neg[:, :], -0.5).then_inc(zeroed, 1)
            pool.memset(minus_one[:, :], -1.0).then_inc(zeroed, 1)
            pool.wait_ge(zeroed, 3)
            pool.affine_select(out=ident[:, :], in_=ident[:, :], compare_op=ALU.not_equal, fill=1.0,
                               base=0, pattern=[[-1, P]], channel_multiplier=1).then_inc(masks, 1)
            pool.memset(strict_f[:, :], 0.0).then_inc(zeroed, 1)
            pool.memset(never_f[:, :], 0.0).then_inc(zeroed, 1)
            pool.memset(tri[:, :], 1.0).then_inc(zeroed, 1)
            pool.memset(cin[:, :, 0:HALO], 0.0).then_inc(zeroed, 1)
            pool.memset(state[:, :, :], 0.0).then_inc(zeroed, 1)
            pool.wait_ge(zeroed, 8)
            pool.affine_select(out=tri[:, :], in_=tri[:, :], compare_op=ALU.is_ge, fill=0.0,
                               base=0, pattern=[[1, P]], channel_multiplier=-1).then_inc(masks, 1)
            pool.affine_select(out=strict_f[:, :], in_=strict_f[:, :], compare_op=ALU.is_ge, fill=1.0,
                               base=0, pattern=[[1, P]], channel_multiplier=-1).then_inc(masks, 1)
            pool.affine_select(out=never_f[:, :], in_=never_f[:, :], compare_op=ALU.is_ge, fill=NEVER,
                               base=0, pattern=[[1, P]], channel_multiplier=-1).then_inc(masks, 1)

            def rms_of(which, n, squares, count):
                pool.wait_ge(squares, count)
                pool.tensor_scalar(rms[:, which, count - 1:count], ssq[:, which, count - 1:count],
                                   1.0 / DM, EPS, ALU.mult, ALU.add).then_inc(ms_rdy, 1)
                pool.wait_ge(ms_rdy, n + 1)
                pool.tensor_tensor(rms[:, which, count - 1:count], rms[:, which, count - 1:count],
                                   half_neg[:, :], ALU.pow).then_inc(rms_rdy, 1)

            for c in range(CPH):
                rms_of(0, c, xsq, c + 1)
            pool.wait_ge(phi, 1)
            pool.tensor_tensor(pair_lo[:, 0, :, :, :].rearrange("p j k f -> p (j k f)"),
                               pair_raw[:, 0, :, :, :].rearrange("p j k f -> p (j k f)"),
                               pair_hi[:, 0, :, :, :].rearrange("p j k f -> p (j k f)").bitcast(F32),
                               ALU.subtract).then_inc(plo, 1)
            pool.wait_ge(masks, 4)
            pool.wait_ge(consts_in, CONSTS * 16)
            pool.tensor_tensor(dskip_diag[:, :, :],
                               ident[:, :].rearrange("p (a q) -> p a q", a=1).to_broadcast([P, H, P]),
                               dskip_b[:, :].rearrange("p (h a) -> p h a", a=1).to_broadcast([P, H, P]),
                               ALU.mult).then_inc(diag_rdy, 1)
            for c in range(CPH, NCH):
                rms_of(0, c, xsq, c + 1)

            def softplus(half):
                done = [SOFT_STEPS * half]

                def step(instruction):
                    instruction.then_inc(soft, 1)
                    done[0] += 1
                    pool.wait_ge(soft, done[0])

                v, e, t, p = (dv[:, i, :, :] for i in range(4))
                dt, a = dt_c[:, half, :, :], a_c[:, :, :]
                pool.wait_ge(dt_exp, half + 1)
                step(pool.tensor_scalar(t, e, 2.0, None, ALU.add))
                step(pool.tensor_tensor(t, t, minus_one[:, :].rearrange("p (c h) -> p c h", c=1)
                                        .to_broadcast([P, CPH, H]), ALU.pow))
                step(pool.tensor_tensor(e, e, t, ALU.mult))
                step(pool.tensor_tensor(t, e, e, ALU.mult))
                step(pool.tensor_scalar(p, t, ATANH[-1], None, ALU.mult))
                for c in ATANH[-2:0:-1]:
                    step(pool.tensor_scalar(p, p, c, None, ALU.add))
                    step(pool.tensor_tensor(p, p, t, ALU.mult))
                step(pool.tensor_scalar(p, p, ATANH[0], 2.0, ALU.add, ALU.mult))
                step(pool.tensor_tensor(p, p, e, ALU.mult))
                step(pool.tensor_scalar(v, v, 0.0, None, ALU.max))
                step(pool.tensor_tensor(dt, p, v, ALU.add))
                pool.wait_ge(nega_rdy, 1)
                step(pool.tensor_tensor(a, dt, per_head(neg_a[:, :]), ALU.mult))
                step(pool.tensor_copy(a_hl[:, half, :, 0, :], a))
                step(pool.tensor_tensor(a_hl[:, half, :, 1, :], a, a_hl[:, half, :, 0, :].bitcast(F32), ALU.subtract))
                assert done[0] == SOFT_STEPS * (half + 1)

            def out_weight_lo(v):
                pool.wait_ge(dhi, v + 1)
                pool.tensor_tensor(wo_lo[:, v, :], down_raw[:, v % 2, :], wo_hi[:, v, :].bitcast(F32), ALU.subtract)\
                    .then_inc(dlo, 1)

            def tri_times_a(n):
                half, c = divmod(n, CPH)
                pool.wait_ge(soft, SOFT_STEPS * (half + 1))
                wait(pool, e_ps, n)
                pool.tensor_tensor(
                    r_hl[:, :, :, :].rearrange("p s h q -> p (s h) q"),
                    tri[:, :].rearrange("p (a q) -> p a q", a=1).to_broadcast([P, 2 * H, P]),
                    a_hl[:, half, c, :, :].bitcast(F32).rearrange("p s (h a) -> p (s h) a", a=1)
                        .to_broadcast([P, 2 * H, P]),
                    ALU.mult).then_inc(r_rdy, 1)

            def decays(n):
                half, c = divmod(n, CPH)
                pool.wait_ge(dec_exp, n + 1)
                wait(pool, xs_rdy, n - 1)
                pool.tensor_tensor(to_end[:, n % 2, :], decay[:, :, P - 1], dt_c[:, half, c, :], ALU.mult)\
                    .then_inc(end_rdy, 1)
                pool.wait_ge(car_exp, n + 1)
                wait(pool, y_ps, n)
                pool.tensor_tensor(ce[:, :, :], carry[:, :, :],
                                   xbc[:, half, 2:CONV, c * P:(c + 1) * P], ALU.mult).then_inc(ce_rdy, 1)

            softplus(0)
            tri_times_a(0)
            for v in range(H):
                out_weight_lo(v)
            tri_times_a(1)
            decays(0)
            for it in range(NCH + 1):
                if it + 2 < NCH:
                    tri_times_a(it + 2)
                if it + 1 < NCH:
                    decays(it + 1)
                if it == 0:
                    softplus(1)
                if 1 <= it:
                    rms_of(1, NCH + it - 1, hsq, it)
                    pool.wait_ge(hid_rdy, it)
                    pool.tensor_tensor(resid[:, it - 1, :], resid[:, it - 1, :], hid[:, :], ALU.add)\
                        .then_inc(hx_rdy, 1)

            for s in range(len(STAGES)):
                for t in range(CPH):
                    n = s * CPH + t
                    pool.wait_ge(mv_rdy, n + 1)
                    pool.tensor_scalar(rstd[:, t:t + 1], mv[:, t, 1:2], EPS, None, ALU.add)\
                        .then_inc(ve_rdy, 1)
                    pool.wait_ge(ve_rdy, n + 1)
                    pool.tensor_tensor(rstd[:, t:t + 1], rstd[:, t:t + 1], half_neg[:, :], ALU.pow)\
                        .then_inc(rstd_rdy, 1)

        @block.tensor
        def _(pe):
            def three(dst, w_hi, w_lo, m_hi, m_lo, start, stop):
                pe.matmul(dst, w_hi, m_hi, start=start, stop=False)
                pe.matmul(dst, w_hi, m_lo, start=False, stop=False)
                return pe.matmul(dst, w_lo, m_hi, start=False, stop=stop)

            def transpose_chunk(dst, src, signal):
                for k in range(KT):
                    last = pe.transpose(dst[:, k * P:(k + 1) * P], src[:, k * P:(k + 1) * P], ident[:, :])
                last.then_inc(signal, 1)

            def x_t(c):
                pe.wait_ge(xn_rdy, c + 1)
                wait(pe, xt_lo, c - 1)
                transpose_chunk([B_E, B_O][c % 2], normed[:, c % 2, :], xt_ps)

            def project(half, i):
                u, j = half * IN_PAIRS + i // 2, i % 2
                n = half * IN_COUNT + i
                pe.wait_ge(plo, u + 1)
                wait(pe, in_free, n if half else n - 1)
                for k in range(KT):
                    last = three(in_bank(half, i)[:, :], pair_hi[:, u % 2, j, k, :], pair_lo[:, u % 2, j, k, :],
                                 act_hi[:, half, k, :], act_lo[:, half, k, :], k == 0, k == KT - 1)
                last.then_inc(in_ps, 1)

            def dt_t(half):
                pe.wait_ge(in_free, half * IN_COUNT + 1)
                wait(pe, dec_exp, 2 * half)
                for c in range(CPH):
                    last = pe.transpose(B_D[:, c * P:(c + 1) * P], dt_row[:, c * P:(c + 1) * P], ident[:, :])
                last.then_inc(dtt_ps, 1)

            def bx_t(n):
                half, c = divmod(n, CPH)
                pe.wait_ge(conv_rdy, half * CONV + 2)
                if n == 0:
                    pe.wait_ge(in_free, IN_COUNT - 1)
                wait(pe, bx_rdy, n)
                for i, tile in enumerate((1, 0)):
                    last = pe.transpose(B_BX[:, i * P:(i + 1) * P], xbc[:, half, tile, c * P:(c + 1) * P],
                                        ident[:, :])
                last.then_inc(bxt_ps, 1)

            def flat(t):
                return t.rearrange("p h q -> p (h q)")

            def scores(n):
                half, c = divmod(n, CPH)
                tok = slice(c * P, (c + 1) * P)
                pe.wait_ge(conv_rdy, (half + 1) * CONV)
                wait(pe, att_mul, n)
                pe.matmul(B_S[:, :], xbc[:, half, 1, tok], xbc[:, half, 2:CONV, tok], start=True, stop=True)\
                    .then_inc(s_ps, 1)
                wait(pe, dec_exp, n)
                if n == 0:
                    pe.wait_ge(dt_sum, 1)
                    pe.wait_ge(ones_rdy, 4)
                if n == 2:
                    pe.wait_ge(dt_sum, 3)
                pe.matmul(B_D[:, :], ident_r[:, :], flat(never[:, :, :]), start=True, stop=False)
                pe.wait_ge(r_rdy, n + 1)
                for i in range(2):
                    last = pe.matmul(B_D[:, :], strict[:, :], flat(r_hl[:, i, :, :]), start=False, stop=i == 1)
                last.then_inc(d_ps, 1)
                if n == 0:
                    pe.wait_ge(xt_lo, NCH)
                wait(pe, car_exp, n)
                wait(pe, h2t_lo, n - 3)
                for i in range(2):
                    last = pe.matmul(B_E[:, :], ones[:, :], flat(r_hl[:, i, :, :]), start=i == 0, stop=i == 1)
                last.then_inc(e_ps, 1)

            def mix(n):
                pe.wait_ge(ce_rdy, n + 1)
                wait(pe, st_rdy, n)
                wait(pe, y_rdy, n)
                if n == 0:
                    pe.wait_ge(zeroed, 8)
                for h in range(H):
                    pe.matmul(B_Y[:, h * P:(h + 1) * P], state[:, h, :], ce[:, h, :],
                              start=h == 0, stop=False, skip_group_check=True)
                pe.wait_ge(att_d, n + 1)
                pe.wait_ge(bx_rdy, n + 1)
                pe.matmul(B_Y[:, :], bx[:, n % 2, 1, :], flat(att[:, n % 2, :, :]), start=False, stop=True,
                          skip_group_check=True).then_inc(y_ps, 1)
                if n < NCH - 1:
                    pe.wait_ge(xs_rdy, n + 1)
                    pe.matmul(B_ST[:, :], bx[:, n % 2, 0, :], flat(xs[:, n % 2, :, :]), start=True, stop=True)\
                        .then_inc(st_ps, 1)

            def out_proj(n):
                if n == 0:
                    pe.wait_ge(dlo, H)
                pe.wait_ge(y_lo_s, n + 1)
                wait(pe, hid_rdy, n)
                for h in range(H):
                    last = three(B_O[:, :], y_hl[:, n % 2, 0, h, :], y_hl[:, n % 2, 1, h, :], wo_hi[:, h, :], wo_lo[:, h, :],
                                 h == 0, h == H - 1)
                last.then_inc(o_ps, 1)

            def h2_t(n):
                pe.wait_ge(h2_rdy, n + 1)
                if n < NCH - 2:
                    pe.wait_ge(car_exp, min(n + 4, NCH))
                else:
                    pe.wait_ge(st_rdy, NCH - 1)
                wait(pe, h2t_lo, n)
                transpose_chunk(h2_bank(n), normed[:, n % 2, :], h2t_ps)

            def fill(it, place):
                for i in BETWEEN.get((it, place), ()):
                    project(1, i)

            pe.wait_ge(masks, 1)
            for c in range(CPH):
                x_t(c)
            pe.wait_ge(xt_lo, CPH)
            for i in range(IN_COUNT):
                project(0, i)
                if i == 1:
                    dt_t(0)
                if 2 <= i <= 8 and i % 2 == 0:
                    x_t(CPH + i // 2 - 1)
            bx_t(0)
            scores(0)
            pe.wait_ge(xt_lo, NCH)
            fill(-1, 2)
            bx_t(1)
            for it in range(NCH):
                if it + 1 < NCH:
                    scores(it + 1)
                fill(it, 0)
                if it == 0:
                    dt_t(1)
                mix(it)
                fill(it, 1)
                if it + 2 < NCH:
                    bx_t(it + 2)
                if it >= 2:
                    h2_t(it - 2)
                if it >= 1:
                    out_proj(it - 1)
                fill(it, 2)

            def gate_up(i, c, half):
                pe.wait_ge(plo, i * 2 + (c + U0 + 1))
                for j, (freed, signal) in enumerate(((silu_rdy, gate_ps), (g_rdy, up_ps))):
                    if c == 0 and j == 0:
                        pe.wait_ge(in_free, NHALF * IN_COUNT)
                    elif c == 0:
                        pe.wait_ge(bx_rdy, NCH)
                    else:
                        pe.wait_ge(freed, i * 2 + c)
                    for k in range(KT):
                        last = three(B_IN[j][:, :], pair_hi[:, c % 2, j, k, :], pair_lo[:, c % 2, j, k, :],
                                     act_hi[:, half, k, :], act_lo[:, half, k, :], k == 0, k == KT - 1)
                    last.then_inc(signal, 1)

            def down(i, c, start, stop):
                pe.wait_ge(dlo, i * 2 + (c + H + 1))
                pe.wait_ge(g_lo_s, i * 2 + (c + 1))
                for t in range(CPH):
                    tok = slice(t * P, (t + 1) * P)
                    last = three(B_ACC[t][:, :], g_hl[c % 2][:, 0, tok], g_hl[c % 2][:, 1, tok],
                                 down_hi[:, c % 2, :], down_lo[:, c % 2, :], start, stop)
                    if stop and t < CPH - 1:
                        last.then_inc(acc_ps, 1)
                last.then_inc(down_used, 1)

            def ln_t(half, part):
                for t in (2 * part, 2 * part + 1):
                    n = half * CPH + t
                    pe.wait_ge(ln_rdy, n + 1)
                    wait(pe, lt_lo, n - 1)
                    transpose_chunk(B_NT[n % 2], resid[:, n, :], lt_ps)

            pe.wait_ge(h2t_lo, CPH)
            gate_up(0, 0, 0)
            h2_t(NCH - 2)
            out_proj(NCH - 1)
            for s, (p0, d0, n, half) in enumerate(STAGES):
                b = BASE[s]
                gate_up(0, b + 1, half)
                if s:
                    pe.wait_ge(acc_free, CPH * s)
                else:
                    h2_t(NCH - 1)
                    pe.wait_ge(h2t_lo, NCH - 2)
                down(0, b, True, False)
                for part, (first, end) in enumerate(loops(s)):
                    with pe.Fori(first, end) as i:
                        for j in range(2):
                            gate_up(i, b + 2 + j, half)
                            down(i, b + 1 + j, False, False)
                    if s in (1, 2) and part < 2:
                        ln_t(s - 1, part)
                for k in range(2 * end + 2, n):
                    gate_up(0, b + k, half)
                    down(0, b + k - 1, False, False)
                if s + 1 < len(STAGES):
                    if s:
                        pe.wait_ge(lt_lo, CPH * s)
                    else:
                        pe.wait_ge(h2t_lo, NCH)
                    gate_up(0, b + n, STAGES[s + 1][3])
                down(0, b + n - 1, False, True)

        @block.scalar
        def _(act):
            def split_pair(i, c):
                act.wait_ge(pair_in[c % 2], i * 16 + 16 * (c // 2 + 1))
                act.activation(pair_hi[:, c % 2, :, :, :].rearrange("p j k f -> p (j k f)"),
                               pair_raw[:, c % 2, :, :, :].rearrange("p j k f -> p (j k f)"), ACT.Copy)\
                    .then_inc(phi, 1)

            def split_down(i, c, dst):
                act.wait_ge(down_in[c % 2], i * 16 + 16 * (c // 2 + 1))
                act.activation(dst, down_raw[:, c % 2, :], ACT.Copy).then_inc(dhi, 1)

            def square(src, which, c, signal):
                wait(act, xsq, NCH * which)
                wait(act, signal, c)
                act.activation(junk[:, :], src, ACT.Square, accum_out=ssq[:, which, c:c + 1])\
                    .then_inc(signal, 1)

            def transposed_hi(ps, count, b, n, signal):
                half, c = divmod(n, CPH)
                act.wait_ge(ps, count)
                act.activation(act_hi[:, half, :, c * P:(c + 1) * P], heads(b), ACT.Copy).then_inc(signal, 1)

            def conv_silu(half, m):
                j = CONV_ORDER[m]
                act.wait_ge(tap_dve, HALO * (half * CONV + m + 1))
                act.activation(xbc[:, half, j, :], xbc[:, half, j, :], ACT.Silu).then_inc(conv_rdy, 1)

            def leave(half, i):
                n = half * IN_COUNT + i
                kind, j = IN_TILES[i]
                act.wait_ge(in_ps, n + 1)
                b = in_bank(half, i)
                if kind == "dt":
                    wait(act, dtt_ps, half)
                    act.activation(dt_row[:, :], b[:, :], ACT.Copy).then_inc(in_free, 1)
                elif kind == "conv":
                    if half:
                        act.wait_ge(tap_dve, HALO * i)
                        act.activation(cin[:, j, 0:HALO], cin[:, j, HT:HT + HALO], ACT.Copy)\
                            .then_inc(halo_rdy, 1)
                        act.wait_ge(halo_rdy, i)
                    act.activation(cin[:, j, HALO:HALO + HT], b[:, :], ACT.Copy).then_inc(cin_rdy, 1)
                    act.activation(xbc[:, half, j, :], b[:, :], ACT.Identity,
                                   scale=cw[:, j, HALO:TAPS], bias=cb[:, j:j + 1]).then_inc(in_free, 1)
                else:
                    act.activation(zs[:, half, j, :], b[:, :], ACT.Silu).then_inc(in_free, 1)

                if i % 2 or i == IN_COUNT - 1:
                    split_pair(0, half * IN_PAIRS + i // 2 + 2)

            def dt_exps(half):
                act.wait_ge(dt_sum, 2 * half + 2)
                act.activation(dv[:, 1, :, :], dv[:, 1, :, :], ACT.Exp).then_inc(dt_exp, 1)

            def exps(n):
                act.wait_ge(d_ps, n + 1)
                wait(act, att_mul, n)
                wait(act, end_rdy, n)
                act.activation(decay[:, :, :], heads(B_D), ACT.Exp).then_inc(dec_exp, 1)
                act.wait_ge(e_ps, n + 1)
                wait(act, ce_rdy, n)
                act.activation(carry[:, :, :], heads(B_E), ACT.Exp).then_inc(car_pre, 1)
                act.wait_ge(car_pre, n + 1)
                wait(act, st_rdy, n - 1)
                act.activation(carry_last[:, n % 2, :], carry[:, :, P - 1], ACT.Copy).then_inc(car_exp, 1)

            def bx_copy(n):
                act.wait_ge(bxt_ps, n + 1)
                wait(act, y_ps, n - 1)
                wait(act, st_ps, n - 1)
                act.activation(bx[:, n % 2, :, :], B_BX[:, 0:2 * P].rearrange("p (i q) -> p i q", i=2), ACT.Copy)\
                    .then_inc(bx_rdy, 1)

            def scale_x(n):
                act.wait_ge(bx_rdy, n + 1)
                act.wait_ge(end_rdy, n + 1)
                wait(act, st_ps, n - 1)
                for h in range(H):
                    last = act.activation(xs[:, n % 2, h, :], bx[:, n % 2, 1, :], ACT.Copy,
                                          scale=to_end[:, n % 2, h:h + 1])
                last.then_inc(xs_rdy, 1)

            def y_hi(n):
                act.wait_ge(y_rdy, n + 1)
                wait(act, o_ps, n - 1)
                act.activation(y_hl[:, n % 2, 0, :, :], y[:, :, :], ACT.Copy).then_inc(y_hi_s, 1)

            def leave_between(it, place):
                for i in BETWEEN.get((it, place), ()):
                    leave(1, i)

            def h2_hi(n):
                transposed_hi(h2t_ps, n + 1, h2_bank(n), n, h2t_hi)

            def square_hid(n):
                act.wait_ge(hid_rdy, n + 1)
                square(hid[:, :], 1, n, hsq)

            for c in range(CPH):
                act.wait_ge(x_in[c], 16)
                square(resid[:, c, :], 0, c, xsq)
            for c in range(CPH):
                transposed_hi(xt_ps, c + 1, [B_E, B_O][c % 2], c, xt_hi)
                if c == 0:
                    split_pair(0, 0)
            split_pair(0, 1)
            act.wait_ge(consts_in, CONSTS * 16)
            act.activation(neg_a[:, :], neg_a[:, :], ACT.Exp).then_inc(aexp_rdy, 1)
            for c in range(CPH, NCH):
                act.wait_ge(x_in[c], 16)
                square(resid[:, c, :], 0, c, xsq)
            for p in range(IN_PAIRS):
                for i in range(2 * p, min(2 * p + 2, IN_COUNT)):
                    leave(0, i)
                if p == 1:
                    dt_exps(0)
                if p == 3:
                    for m in range(CONV - 1):
                        conv_silu(0, m)
                if p == 4:
                    conv_silu(0, CONV - 1)
                if p in (3, 4):
                    for v in (2 * p - 6, 2 * p - 5):
                        split_down(0, v, wo_hi[:, v, :])
                if 1 <= p <= CPH:
                    transposed_hi(xt_ps, CPH + p, [B_E, B_O][(p - 1) % 2], CPH + p - 1, xt_hi)
            bx_copy(0)
            exps(0)
            leave_between(-1, 2)
            scale_x(0)
            bx_copy(1)
            for it in range(NCH):
                if it + 1 < NCH:
                    exps(it + 1)
                leave_between(it, 0)
                if it + 1 < NCH - 1:
                    scale_x(it + 1)
                if it == 0:
                    dt_exps(1)
                leave_between(it, 1)
                if it == 2:
                    for m in range(3, CONV):
                        conv_silu(1, m)
                if it + 2 < NCH:
                    bx_copy(it + 2)
                y_hi(it)
                if it >= 2:
                    h2_hi(it - 2)
                if it >= 1:
                    square_hid(it - 1)
                leave_between(it, 2)
                if it == 1:
                    for m in range(3):
                        conv_silu(1, m)
                if it == 4:
                    split_down(0, H, down_hi[:, 0, :])

            def gated_step(i, c):
                act.wait_ge(gate_ps, i * 2 + (c + 1))
                if c:
                    act.wait_ge(g_rdy, i * 2 + c)
                act.activation(gate_s, B_IN[0][:, :], ACT.Silu).then_inc(silu_rdy, 1)
                if c < STEPS - 2:
                    act.wait_ge(up_ps, i * 2 + (c + 1))
                    split_pair(i, c + U0 + 2)
                act.wait_ge(g_rdy, i * 2 + (c + 1))
                act.activation(g_hl[c % 2][:, 0, :], gated, ACT.Copy).then_inc(g_hi_s, 1)
                if c < STEPS - 1:
                    if c:
                        act.wait_ge(down_used, i * 2 + c)
                    split_down(i, c + H + 1, down_hi[:, (c + 1) % 2, :])

            def ln_hi(half, part):
                for t in (2 * part, 2 * part + 1):
                    n = half * CPH + t
                    transposed_hi(lt_ps, n + 1, B_NT[n % 2], n, lt_hi)

            for s, (p0, d0, n, half) in enumerate(STAGES):
                b = BASE[s]
                if s == 0:
                    act.wait_ge(att_mul, NCH)
                    act.wait_ge(end_rdy, NCH)
                gated_step(0, b)
                if s == 0:
                    h2_hi(NCH - 2)
                    square_hid(NCH - 1)
                gated_step(0, b + 1)
                if s == 0:
                    h2_hi(NCH - 1)
                for part, (first, end) in enumerate(loops(s)):
                    with act.Fori(first, end) as i:
                        for j in range(2):
                            gated_step(i, b + 2 + j)
                    if s in (1, 2) and part < 2:
                        ln_hi(s - 1, part)
                for k in range(2 * end + 2, n):
                    gated_step(0, b + k)

        @block.vector
        def _(dve):
            def f32(t):
                return t.bitcast(F32)

            def pair_rest(i, c):
                dve.wait_ge(phi, i * 2 + (c + 1))
                dve.tensor_tensor(pair_lo[:, c % 2, :, :, :].rearrange("p j k f -> p (j k f)"),
                                  pair_raw[:, c % 2, :, :, :].rearrange("p j k f -> p (j k f)"),
                                  f32(pair_hi[:, c % 2, :, :, :].rearrange("p j k f -> p (j k f)")),
                                  ALU.subtract).then_inc(plo, 1)

            def down_rest(i, c, hi, lo):
                dve.wait_ge(dhi, i * 2 + (c + 1))
                dve.tensor_tensor(lo, down_raw[:, c % 2, :], f32(hi), ALU.subtract).then_inc(dlo, 1)

            def x_norm(c):
                dve.wait_ge(rms_rdy, c + 1)
                if c == 0:
                    dve.wait_ge(ln1_in, 16)
                wait(dve, xt_ps, c - 1)
                dve.scalar_tensor_tensor(out=normed[:, c % 2, :], in0=resid[:, c, :], scalar=rms[:, 0, c:c + 1],
                                         in1=ln_b[:, :], op0=ALU.mult, op1=ALU.mult).then_inc(xn_rdy, 1)

            def transposed_lo(hi_signal, count, b, n, signal):
                half, c = divmod(n, CPH)
                tok = slice(c * P, (c + 1) * P)
                dve.wait_ge(hi_signal, count)
                dve.tensor_tensor(act_lo[:, half, :, tok], heads(b), f32(act_hi[:, half, :, tok]), ALU.subtract)\
                    .then_inc(signal, 1)

            def taps(half, m):
                j = CONV_ORDER[m]
                dve.wait_ge(in_free, half * IN_COUNT + m + 2)
                if half == 0 and m == 0:
                    dve.wait_ge(zeroed, 8)
                for k in range(HALO):
                    wait(dve, tap_dve, HALO * (half * CONV + m) + k)
                    dve.scalar_tensor_tensor(out=xbc[:, half, j, :], in0=cin[:, j, k:k + HT],
                                             scalar=cw[:, j, k:k + 1], in1=xbc[:, half, j, :],
                                             op0=ALU.mult, op1=ALU.add).then_inc(tap_dve, 1)

            def dt_bias_sum(half):
                dve.wait_ge(dtt_ps, half + 1)
                if half == 0:
                    dve.wait_ge(consts_in, CONSTS * 16)
                wait(dve, soft, SOFT_STEPS * half)
                v, e = dv[:, 0, :, :], dv[:, 1, :, :]
                dve.tensor_tensor(v, heads(B_D)[:, :, 0:H], per_head(dtb_b[:, :]), ALU.add).then_inc(dt_sum, 1)
                dve.wait_ge(dt_sum, 2 * half + 1)
                dve.scalar_tensor_tensor(out=e, in0=v, scalar=-1.0, in1=v, op0=ALU.mult, op1=ALU.min)\
                    .then_inc(dt_sum, 1)

            def attention(n):
                half, c = divmod(n, CPH)
                dve.wait_ge(s_ps, n + 1)
                dve.wait_ge(dec_exp, n + 1)
                if c == 0:
                    dve.wait_ge(soft, SOFT_STEPS * (half + 1))
                wait(dve, y_ps, n - 1)
                for h in range(H):
                    last = dve.scalar_tensor_tensor(out=att[:, n % 2, h, :], in0=B_S[:, h * P:(h + 1) * P],
                                                    scalar=dt_c[:, half, c, h:h + 1], in1=decay[:, h, :],
                                                    op0=ALU.mult, op1=ALU.mult)
                last.then_inc(att_mul, 1)
                dve.wait_ge(att_mul, n + 1)
                if n == 0:
                    dve.wait_ge(diag_rdy, 1)
                dve.tensor_tensor(att[:, n % 2, :, :], att[:, n % 2, :, :], dskip_diag[:, :, :], ALU.add)\
                    .then_inc(att_d, 1)

            def y_gate(n):
                half, c = divmod(n, CPH)
                dve.wait_ge(in_free, (half + 1) * IN_COUNT)
                dve.wait_ge(y_ps, n + 1)
                wait(dve, y_lo_s, n)
                dve.tensor_tensor(y[:, :, :], heads(B_Y), zs[:, half, :, c * P:(c + 1) * P], ALU.mult)\
                    .then_inc(y_rdy, 1)

            def y_rest(n):
                dve.wait_ge(y_hi_s, n + 1)
                dve.tensor_tensor(y_hl[:, n % 2, 1, :, :], y[:, :, :], f32(y_hl[:, n % 2, 0, :, :]), ALU.subtract)\
                    .then_inc(y_lo_s, 1)

            def update_state(n):
                dve.wait_ge(st_ps, n + 1)
                dve.wait_ge(car_exp, n + 1)
                wait(dve, st_rdy, n)
                for h in range(H):
                    last = dve.scalar_tensor_tensor(out=state[:, h, :], in0=state[:, h, :],
                                                    scalar=carry_last[:, n % 2, h:h + 1],
                                                    in1=B_ST[:, h * P:(h + 1) * P], op0=ALU.mult, op1=ALU.add)
                last.then_inc(st_rdy, 1)

            def hidden(n):
                dve.wait_ge(o_ps, n + 1)
                wait(dve, hx_rdy, n)
                wait(dve, hsq, n)
                wait(dve, h2_rdy, n)
                dve.tensor_tensor(hid[:, :], B_O[:, :], resid[:, n, :], ALU.add).then_inc(hid_rdy, 1)

            def h2_norm(n):
                dve.wait_ge(rms_rdy, NCH + n + 1)
                dve.wait_ge(ln2_in, 16)
                wait(dve, h2t_ps, n - 1)
                if n < 2:
                    dve.wait_ge(xt_ps, NCH)
                dve.scalar_tensor_tensor(out=normed[:, n % 2, :], in0=hid[:, :], scalar=rms[:, 1, n:n + 1],
                                         in1=ln_b[:, :], op0=ALU.mult, op1=ALU.mult).then_inc(h2_rdy, 1)

            def h2_lo(n):
                transposed_lo(h2t_hi, n + 1, h2_bank(n), n, h2t_lo)

            def tiles_rest(it, place):
                for i in BETWEEN.get((it, place), ()):
                    if i % 2 or i == IN_COUNT - 1:
                        pair_rest(0, IN_PAIRS + i // 2 + 2)

            x_norm(0)
            x_norm(1)
            for c in range(CPH):
                if c + 2 < CPH:
                    x_norm(c + 2)
                transposed_lo(xt_hi, c + 1, [B_E, B_O][c % 2], c, xt_lo)
            dve.wait_ge(plo, 1)
            pair_rest(0, 1)
            x_norm(CPH)
            x_norm(CPH + 1)
            dve.wait_ge(masks, 4)
            dve.tensor_copy(strict[:, :], strict_f[:, :]).then_inc(ones_rdy, 1)
            dve.tensor_copy(ident_r[:, :], ident[:, :]).then_inc(ones_rdy, 1)
            dve.tensor_scalar(ones[:, :], strict_f[:, :], 0.0, 1.0, ALU.mult, ALU.add).then_inc(ones_rdy, 1)
            dve.tensor_copy(never[:, :, :], never_f[:, :].rearrange("p (a q) -> p a q", a=1)
                            .to_broadcast([P, H, P])).then_inc(ones_rdy, 1)
            dve.wait_ge(aexp_rdy, 1)
            dve.tensor_scalar(neg_a[:, :], neg_a[:, :], -1.0, None, ALU.mult).then_inc(nega_rdy, 1)
            dve.wait_ge(nega_rdy, 1)
            for p in range(IN_PAIRS):
                if p == 0:
                    dt_bias_sum(0)
                for m in (2 * p - 1, 2 * p):
                    if 0 <= m < CONV:
                        taps(0, m)
                pair_rest(0, p + 2)
                if 1 <= p <= CPH:
                    transposed_lo(xt_hi, CPH + p, [B_E, B_O][(p - 1) % 2], CPH + p - 1, xt_lo)
                if 1 <= p < 3:
                    x_norm(CPH + p + 1)
            attention(0)
            tiles_rest(-1, 2)
            for it in range(NCH):
                if it >= 2:
                    h2_norm(it - 2)
                if it + 1 < NCH:
                    attention(it + 1)
                if it == 0:
                    taps(1, 0)
                    dt_bias_sum(1)
                elif it == 1:
                    taps(1, 2)
                elif it == 2:
                    taps(1, 5)
                tiles_rest(it, 0)
                y_gate(it)
                if it + 1 < NCH:
                    update_state(it)
                y_rest(it)
                tiles_rest(it, 1)
                if it == 0:
                    taps(1, 1)
                if it >= 2:
                    h2_lo(it - 2)
                if it >= 1:
                    hidden(it - 1)
                if it == 1:
                    taps(1, 3)
                    taps(1, 4)
                tiles_rest(it, 2)
                if it == 4:
                    down_rest(0, H, down_hi[:, 0, :], down_lo[:, 0, :])

            def gated_step(i, c):
                dve.wait_ge(silu_rdy, i * 2 + (c + 1))
                dve.wait_ge(up_ps, i * 2 + (c + 1))
                if c:
                    dve.wait_ge(g_lo_s, i * 2 + c)
                dve.tensor_tensor(gated, B_IN[1][:, :], gate_s, ALU.mult).then_inc(g_rdy, 1)
                if c < STEPS - 2:
                    pair_rest(i, c + U0 + 2)
                dve.wait_ge(g_hi_s, i * 2 + (c + 1))
                dve.tensor_tensor(g_hl[c % 2][:, 1, :], gated, f32(g_hl[c % 2][:, 0, :]), ALU.subtract)\
                    .then_inc(g_lo_s, 1)
                if c < STEPS - 1:
                    down_rest(i, c + H + 1, down_hi[:, (c + 1) % 2, :], down_lo[:, (c + 1) % 2, :])

            def join(s, t):
                n = STAGES[s][3] * CPH + t
                if t < CPH - 1:
                    dve.wait_ge(acc_ps, s * (CPH - 1) + t + 1)
                else:
                    dve.wait_ge(down_used, BASE[s] + STAGES[s][2])
                dve.wait_ge(hx_rdy, NCH)
                dve.tensor_tensor(resid[:, n, :], B_ACC[t][:, :], resid[:, n, :], ALU.add).then_inc(acc_free, 1)

            def moments(s, t):
                count = s * CPH + t + 1
                dve.wait_ge(acc_free, count)
                dve.bn_stats(bn[:, t, :], resid[:, STAGES[s][3] * CPH + t, :]).then_inc(bn_rdy, 1)
                dve.wait_ge(bn_rdy, count)
                dve.bn_aggr(mv[:, t, :], bn[:, t, :]).then_inc(mv_rdy, 1)

            def ln_apply(s, t):
                n = STAGES[s][3] * CPH + t
                dve.wait_ge(rstd_rdy, s * CPH + t + 1)
                dve.tensor_scalar(resid[:, n, :], resid[:, n, :], mv[:, t, 0:1], rstd[:, t:t + 1],
                                  ALU.subtract, ALU.mult).then_inc(ln_rdy, 1)

            def ln_lo(half, part):
                for t in (2 * part, 2 * part + 1):
                    n = half * CPH + t
                    transposed_lo(lt_hi, n + 1, B_NT[n % 2], n, lt_lo)

            h2_norm(NCH - 2)
            for s, (p0, d0, n, half) in enumerate(STAGES):
                b = BASE[s]
                gated_step(0, b)
                if s:
                    for t in range(CPH):
                        join(s - 1, t)
                    for t in range(CPH):
                        moments(s - 1, t)
                else:
                    h2_lo(NCH - 2)
                    hidden(NCH - 1)
                    h2_norm(NCH - 1)
                gated_step(0, b + 1)
                if s:
                    for t in range(CPH):
                        ln_apply(s - 1, t)
                else:
                    h2_lo(NCH - 1)
                for part, (first, end) in enumerate(loops(s)):
                    with dve.Fori(first, end) as i:
                        for j in range(2):
                            gated_step(i, b + 2 + j)
                    if s in (1, 2) and part < 2:
                        ln_lo(s - 1, part)
                for k in range(2 * end + 2, n):
                    gated_step(0, b + k)
            for t in range(CPH + 1):
                if t < CPH:
                    join(s, t)
                    moments(s, t)
                if t:
                    ln_apply(s, t - 1)


def loops(s):
    pairs = (STAGES[s][2] - 2) // 2 - (s == len(STAGES) - 1)
    cuts = [0, pairs // 3, 2 * (pairs // 3), pairs] if s in (1, 2) else [0, pairs]
    return list(zip(cuts, cuts[1:]))


def _feature_tiles(w, tiles):
    padded = np.zeros((tiles * P, DM), w.dtype)
    padded[:w.shape[0]] = w
    return padded.reshape(tiles, P, KT, P).transpose(0, 3, 2, 1)


def _down_tiles(w, tiles):
    padded = np.zeros((tiles * P, DM), w.dtype)
    padded[:w.shape[1]] = w.T
    return padded.reshape(tiles, P, DM)


def kernel(**inputs):
    import concourse.bacc as bacc
    from concourse.bass_utils import run_bass_kernel_spmd

    a = {k[3:]: np.asarray(v) for k, v in inputs.items()}
    w_in = _feature_tiles(a["attn_w_in"], 11)
    row = {"z": 0, "conv": H, "dt": 10}
    blank = np.zeros_like(w_in[0])
    firsts = [blank if kind == "pad" else w_in[row[kind] + j] for kind, j in IN_TILES]
    projections = np.stack(firsts).reshape(IN_PAIRS, 2, P, KT, P)
    mlp = np.stack([_feature_tiles(a[f"attn_{n}_w"], T_MLP) for n in ("gate", "up")], axis=1)
    ffn = np.stack([_feature_tiles(a[f"ffn_W_{n}"], T_FFN) for n in ("gate", "up")], axis=1)
    arrays = {
        "x": a["attn_hidden_states"].reshape(NCH, P, DM),
        "pairs": np.concatenate([projections, mlp, ffn]).transpose(0, 2, 1, 3, 4),
        "downs": np.concatenate([_down_tiles(a["attn_w_out"], H), _down_tiles(a["attn_down_w"], T_MLP),
                                 _down_tiles(a["ffn_W_down"], T_FFN)]),
        "conv_w": a["attn_conv_w"].reshape(CONV, P, TAPS).transpose(1, 0, 2),
        "conv_b": a["attn_conv_b"].reshape(CONV, P).T,
        "a_log": a["attn_A_log"].reshape(1, H),
        "d_skip": a["attn_D"].reshape(1, H),
        "dt_bias": a["attn_dt_bias"].reshape(1, H),
        "ln1": a["attn_ln1_w"].reshape(1, DM),
        "ln2": a["attn_ln2_w"].reshape(1, DM),
    }
    arrays = {f"in_{k}": np.ascontiguousarray(v) for k, v in arrays.items()}
    nc = bacc.Bacc("TRN2", target_bir_lowering=False, num_devices=1)
    args = [nc.dram_tensor(k, v.shape, F32, kind="ExternalInput").ap() for k, v in arrays.items()]
    out = nc.dram_tensor("out", (NCH, P, DM), F32, kind="ExternalOutput").ap()
    build(nc, *args, out)
    result = run_bass_kernel_spmd(nc, [arrays], core_ids=[0])
    return result.results[0]["out"].reshape(1, L, DM)
```

```python
from contextlib import ExitStack

import numpy as np

import concourse.bass as bass
from concourse import mybir

F32 = mybir.dt.float32
F32R = mybir.dt.float32r
ALU = mybir.AluOpType
ACT = mybir.ActivationFunctionType

P = 128
L = 1024
DM = 512
KT = DM // P
H = 4
NCH = L // P
NHALF = 2
CPH = NCH // NHALF
HT = L // NHALF
TAPS = 4
HALO = TAPS - 1
CONV = 6
EPS = 1e-5
NEVER = -1e30
F_MLP, F_FFN = 1792, 1376
T_MLP = F_MLP // P
T_FFN = -(-F_FFN // P)
IN_TILES = [("dt", 0), ("conv", 1), ("conv", 0), ("conv", 2), ("conv", 3), ("conv", 4),
            ("conv", 5), ("z", 0), ("z", 1), ("z", 2), ("z", 3), ("pad", 0)]
IN_PAIRS = len(IN_TILES) // 2
STAGES = [(IN_PAIRS, H, T_MLP, 0), (IN_PAIRS, H, T_MLP, 1),
          (IN_PAIRS + T_MLP, H + T_MLP, T_FFN, 0), (IN_PAIRS + T_MLP, H + T_MLP, T_FFN, 1)]
BASE = [0, T_MLP, 2 * T_MLP, 2 * T_MLP + T_FFN]
STEPS = 2 * (T_MLP + T_FFN)
U0 = NHALF * IN_PAIRS
CONSTS = 5
SOFT_STEPS = 24
BETWEEN = {(-1, 4): 0, (0, 0): 1, (0, 1): 2, (1, 0): 3, (1, 1): 4, (1, 2): 5,
           (2, 0): 6, (2, 1): 7, (2, 2): 8, (2, 3): 9, (2, 4): 10}
BETWEEN_BANK = [0, 0, 0, 0, 1, 0, 0, 1, 0, 1, 0]
CONV_ORDER = [j for kind, j in IN_TILES if kind == "conv"]
IN_COUNT = len(IN_TILES) - 1
WARM_UP = 18
ATANH = [1.0 / (2 * n + 1) for n in range(8)]


def build(nc, x, pairs, downs, conv_w, conv_b, a_log, d_skip, dt_bias, ln1, ln2, out):
    ctx = ExitStack()
    with ctx:
        def sb(name, shape, dt=F32):
            return ctx.enter_context(nc.sbuf_tensor(name, shape, dt))

        def sem(name):
            return ctx.enter_context(nc.semaphore(name))

        resid = sb("resid", [P, NCH, DM])
        act_hi = sb("act_hi", [P, NHALF, KT, HT], F32R)
        act_lo = sb("act_lo", [P, NHALF, KT, HT], F32R)
        zs = sb("zs", [P, NHALF, H, HT])
        cin = sb("cin", [P, CONV, HALO + HT])
        xbc = sb("xbc", [P, NHALF, CONV, HT])
        wo_hi = sb("wo_hi", [P, H, DM], F32R)
        wo_lo = sb("wo_lo", [P, H, DM], F32R)
        pair_raw = sb("pair_raw", [P, 2, 2, KT, P])
        pair_hi = sb("pair_hi", [P, 2, 2, KT, P], F32R)
        pair_lo = sb("pair_lo", [P, 2, 2, KT, P], F32R)
        down_raw = sb("down_raw", [P, 2, DM])
        down_hi = sb("down_hi", [P, 2, DM], F32R)
        down_lo = sb("down_lo", [P, 2, DM], F32R)

        ident = sb("ident", [P, P])
        tri = sb("tri", [P, P])
        strict_f = sb("strict_f", [P, P])
        strict = sb("strict", [P, P], F32R)
        ident_r = sb("ident_r", [P, P], F32R)
        never_f = sb("never_f", [P, P])
        never = sb("never", [P, H, P], F32R)
        ones = sb("ones", [P, P], F32R)
        ln_b = sb("ln_b", [P, DM])
        dskip_b = sb("dskip_b", [P, H])
        dskip_diag = sb("dskip_diag", [P, H, P])
        dtb_b = sb("dtb_b", [P, H])
        neg_a = sb("neg_a", [P, H])
        cw = sb("cw", [P, CONV, TAPS])
        cb = sb("cb", [P, CONV])
        half_neg = sb("half_neg", [P, 1])
        minus_one = sb("minus_one", [P, 1])

        dt_row = sb("dt_row", [P, HT])
        dv = sb("dv", [P, 6, CPH, H])
        dt_c = sb("dt_c", [P, NHALF, CPH, H])
        a_c = sb("a_c", [P, CPH, H])
        a_hl = sb("a_hl", [P, NHALF, CPH, 2, H], F32R)

        bx = sb("bx", [P, 2, 2, P])
        r_hl = sb("r_hl", [P, 2, H, P], F32R)
        decay = sb("decay", [P, H, P])
        carry = sb("carry", [P, H, P])
        carry_last = sb("carry_last", [P, 2, H])
        ce = sb("ce", [P, H, P])
        att = sb("att", [P, 2, H, P])
        to_end = sb("to_end", [P, 2, H])
        xs = sb("xs", [P, 2, H, P])
        state = sb("state", [P, H, P])
        y = sb("y", [P, H, P])
        y_hl = sb("y_hl", [P, 2, 2, H, P], F32R)
        hid = sb("hid", [P, DM])
        normed = sb("normed", [P, 2, DM])
        junk = sb("junk", [P, DM], mybir.dt.bfloat16)
        ssq = sb("ssq", [P, 2, NCH])
        rms = sb("rms", [P, 2, NCH])
        bn = sb("bn", [P, CPH, 6])
        mv = sb("mv", [P, CPH, 2])
        rstd = sb("rstd", [P, CPH])
        shift = sb("shift", [P, CPH])
        gate_s = decay[:, :, :].rearrange("p h q -> p (h q)")
        gated = att[:, 0, :, :].rearrange("p h q -> p (h q)")
        g_hl = [r_hl[:, :, :, :].rearrange("p s h q -> p s (h q)"),
                y_hl[:, 0, :, :, :].rearrange("p s h q -> p s (h q)")]

        bank = [ctx.enter_context(nc.psum_tensor(f"bank{i}", [P, DM], F32)) for i in range(8)]
        B_IN = bank[0:2]
        B_S, B_D, B_E, B_Y, B_ST, B_O = bank[2:8]
        FIRST = [bank[0], B_D]
        B_ACC = bank[2:6]
        B_BX = bank[1]
        B_NT = [bank[6], bank[7]]

        def in_bank(half, i):
            return B_IN[BETWEEN_BANK[i] if half else i % 2]

        def x_bank(c):
            return [B_E, B_O, B_Y, B_ST][c] if c < CPH else [B_E, B_O][c % 2]

        def heads(b):
            return b[:, :].rearrange("p (h q) -> p h q", h=H)

        consts_in, ln1_in, ln2_in = sem("consts_in"), sem("ln1_in"), sem("ln2_in")
        x_in = [sem(f"x_in{c}") for c in range(NCH)]
        pair_in = [sem(f"pair_in{i}") for i in range(2)]
        down_in = [sem(f"down_in{i}") for i in range(2)]
        zeroed, masks, ones_rdy, diag_rdy, nega_rdy, aexp_rdy = map(
            sem, ("zeroed", "masks", "ones_rdy", "diag_rdy", "nega_rdy", "aexp_rdy"))
        phi, plo, dhi, dlo, down_used = map(
            sem, ("pair_hi_rdy", "pair_lo_rdy", "down_hi_rdy", "down_lo_rdy", "down_used"))
        xsq, hsq, ms_rdy, rms_rdy, xn_rdy, xt_ps, xt_hi, xt_lo = map(
            sem, ("xsq", "hsq", "ms_rdy", "rms_rdy", "xn_rdy", "xt_ps", "xt_hi", "xt_lo"))
        first_hi, first_lo = sem("first_tile_hi"), sem("first_tile_lo")
        in_ps, in_free = sem("in_ps"), sem("in_free")
        cin_rdy, halo_rdy, tap_dve, conv_rdy, car_pre = map(
            sem, ("cin_rdy", "halo_rdy", "tap_dve", "conv_rdy", "car_pre"))
        dtt_ps, dt_sum, soft, dt_exp = map(sem, ("dtt_ps", "dt_sum", "soft", "dt_exp"))
        bxt_ps, bx_rdy = sem("bxt_ps"), sem("bx_rdy")
        r_rdy, s_ps, d_ps, e_ps, dec_exp, car_exp, end_rdy = map(
            sem, ("r_rdy", "s_ps", "d_ps", "e_ps", "dec_exp", "car_exp", "end_rdy"))
        att_mul, att_d, ce_rdy, xs_rdy = map(sem, ("att_mul", "att_d", "ce_rdy", "xs_rdy"))
        y_ps, st_ps, st_rdy, y_rdy, y_hi_s, y_lo_s = map(
            sem, ("y_ps", "st_ps", "state_rdy", "y_rdy", "y_hi_rdy", "y_lo_rdy"))
        o_ps, hid_rdy, hx_rdy, h2_rdy, h2t_ps, h2t_hi, h2t_lo = map(
            sem, ("o_ps", "hid_rdy", "hx_rdy", "h2_rdy", "h2t_ps", "h2t_hi", "h2t_lo"))
        up_ps, gate_ps, silu_rdy, g_rdy, g_hi_s, g_lo_s = map(
            sem, ("up_ps", "gate_ps", "silu_rdy", "g_rdy", "g_hi_rdy", "g_lo_rdy"))
        acc_ps, acc_free, bn_rdy, mv_rdy, ve_rdy, rstd_rdy, ln_rdy = map(
            sem, ("acc_ps", "acc_free", "bn_rdy", "mv_rdy", "ve_rdy", "rstd_rdy", "ln_rdy"))
        lt_ps, lt_hi, lt_lo = map(sem, ("lt_ps", "lt_hi", "lt_lo"))
        minus_mean, shift_rdy, act_ln_rdy = sem("minus_mean"), sem("shift_rdy"), sem("act_ln_rdy")
        out_done = sem("out_done")

        def per_head(t):
            return t.rearrange("p (a h) -> p a h", a=1).to_broadcast([P, CPH, H])

        def wait(eng, s, value):
            if not isinstance(value, int) or value > 0:
                eng.wait_ge(s, value)

        block = ctx.enter_context(nc.Block())

        @block.sync
        def _(sp):
            def load_pair(u, tile, slot):
                wait(sp, plo, u - 1)
                sp.dma_start(pair_raw[:, slot, :, :, :], pairs[tile]).then_inc(pair_in[slot], 16)

            def load_down(v, tile, slot):
                wait(sp, dlo, v - 1)
                sp.dma_start(down_raw[:, slot, :], downs[tile]).then_inc(down_in[slot], 16)

            for c in range(CPH):
                sp.dma_start(resid[:, c, :], x[c]).then_inc(x_in[c], 16)
                if c == 0:
                    sp.dma_start(ln_b[:, :], ln1.to_broadcast([P, DM])).then_inc(ln1_in, 16)
            load_pair(0, 0, 0)
            load_pair(1, 1, 1)
            for dst, src in ((cw[:, :, :], conv_w), (cb[:, :], conv_b),
                             (dtb_b[:, :], dt_bias.to_broadcast([P, H])),
                             (neg_a[:, :], a_log.to_broadcast([P, H])),
                             (dskip_b[:, :], d_skip.to_broadcast([P, H]))):
                sp.dma_start(dst, src).then_inc(consts_in, 16)
            for c in range(CPH, NCH):
                sp.dma_start(resid[:, c, :], x[c]).then_inc(x_in[c], 16)
            load_down(0, 0, 0)
            load_down(1, 1, 1)
            for u in range(2, U0 + 2):
                load_pair(u, u % IN_PAIRS if u < U0 else IN_PAIRS + u - U0, u % 2)
                if u == 9:
                    sp.wait_ge(xn_rdy, NCH)
                    sp.dma_start(ln_b[:, :], ln2.to_broadcast([P, DM])).then_inc(ln2_in, 16)
                if u == 7:
                    load_down(2, 2, 0)
                    load_down(3, 3, 1)
            load_down(H, H, 0)

            for s, (p0, d0, n, half) in enumerate(STAGES):
                b = BASE[s]
                looped = (n - 2) // 2
                with sp.Fori(0, looped) as i:
                    for j in range(2):
                        load_pair(i * 2 + (U0 + b + j + 2), i * 2 + (p0 + j + 2), (b + j) % 2)
                        load_down(i * 2 + (H + b + j + 1), i * 2 + (d0 + j + 1), (b + j + 1) % 2)
                for k in range(2 * looped, n):
                    g = b + k
                    following = STAGES[s + 1] if s + 1 < len(STAGES) else None
                    if k + 2 < n:
                        load_pair(U0 + g + 2, p0 + k + 2, g % 2)
                    elif following:
                        load_pair(U0 + g + 2, following[0] + k + 2 - n, g % 2)
                    if k + 1 < n:
                        load_down(H + g + 1, d0 + k + 1, (g + 1) % 2)
                    elif following:
                        load_down(H + g + 1, following[1], (g + 1) % 2)
            for half in range(NHALF):
                for t in range(CPH):
                    if half == 0:
                        sp.wait_ge(ln_rdy, NHALF * CPH + t + 1)
                    elif t < CPH - 1:
                        sp.wait_ge(act_ln_rdy, t + 1)
                    else:
                        sp.wait_ge(ln_rdy, (NHALF + 1) * CPH + 1)
                    sp.dma_start(out[half * CPH + t], resid[:, half * CPH + t, :]).then_inc(out_done, 16)
            sp.wait_ge(out_done, 16 * NCH)

        @block.gpsimd
        def _(pool):
            pool.memset(ident[:, :], 0.0).then_inc(zeroed, 1)
            pool.memset(half_neg[:, :], -0.5).then_inc(zeroed, 1)
            pool.memset(minus_one[:, :], -1.0).then_inc(zeroed, 1)
            pool.wait_ge(zeroed, 3)
            pool.affine_select(out=ident[:, :], in_=ident[:, :], compare_op=ALU.not_equal, fill=1.0,
                               base=0, pattern=[[-1, P]], channel_multiplier=1).then_inc(masks, 1)
            pool.memset(strict_f[:, :], 0.0).then_inc(zeroed, 1)
            pool.memset(never_f[:, :], 0.0).then_inc(zeroed, 1)
            pool.memset(tri[:, :], 1.0).then_inc(zeroed, 1)
            pool.memset(cin[:, :, 0:HALO], 0.0).then_inc(zeroed, 1)
            pool.memset(state[:, :, :], 0.0).then_inc(zeroed, 1)
            pool.wait_ge(zeroed, 8)
            pool.affine_select(out=tri[:, :], in_=tri[:, :], compare_op=ALU.is_ge, fill=0.0,
                               base=0, pattern=[[1, P]], channel_multiplier=-1).then_inc(masks, 1)
            pool.affine_select(out=strict_f[:, :], in_=strict_f[:, :], compare_op=ALU.is_ge, fill=1.0,
                               base=0, pattern=[[1, P]], channel_multiplier=-1).then_inc(masks, 1)
            pool.affine_select(out=never_f[:, :], in_=never_f[:, :], compare_op=ALU.is_ge, fill=NEVER,
                               base=0, pattern=[[1, P]], channel_multiplier=-1).then_inc(masks, 1)

            def rms_of(which, n, squares, count):
                pool.wait_ge(squares, count)
                pool.tensor_scalar(rms[:, which, count - 1:count], ssq[:, which, count - 1:count],
                                   1.0 / DM, EPS, ALU.mult, ALU.add).then_inc(ms_rdy, 1)
                pool.wait_ge(ms_rdy, n + 1)
                pool.tensor_tensor(rms[:, which, count - 1:count], rms[:, which, count - 1:count],
                                   half_neg[:, :], ALU.pow).then_inc(rms_rdy, 1)

            for c in range(CPH):
                rms_of(0, c, xsq, c + 1)
            for j, (hi_signal, signal) in enumerate(((first_hi, first_lo), (phi, plo))):
                pool.wait_ge(hi_signal, 1)
                pool.tensor_tensor(pair_lo[:, 0, j, :, :], pair_raw[:, 0, j, :, :],
                                   pair_hi[:, 0, j, :, :].bitcast(F32), ALU.subtract).then_inc(signal, 1)
            pool.wait_ge(masks, 4)
            pool.wait_ge(consts_in, CONSTS * 16)
            pool.tensor_tensor(dskip_diag[:, :, :],
                               ident[:, :].rearrange("p (a q) -> p a q", a=1).to_broadcast([P, H, P]),
                               dskip_b[:, :].rearrange("p (h a) -> p h a", a=1).to_broadcast([P, H, P]),
                               ALU.mult).then_inc(diag_rdy, 1)
            for c in range(CPH, NCH):
                rms_of(0, c, xsq, c + 1)

            def softplus(half):
                done = [SOFT_STEPS * half]

                def step(instruction):
                    instruction.then_inc(soft, 1)
                    done[0] += 1
                    pool.wait_ge(soft, done[0])

                v, e, t, p = (dv[:, i, :, :] for i in range(4))
                dt, a = dt_c[:, half, :, :], a_c[:, :, :]
                pool.wait_ge(dt_exp, half + 1)
                step(pool.tensor_scalar(t, e, 2.0, None, ALU.add))
                step(pool.tensor_tensor(t, t, minus_one[:, :].rearrange("p (c h) -> p c h", c=1)
                                        .to_broadcast([P, CPH, H]), ALU.pow))
                step(pool.tensor_tensor(e, e, t, ALU.mult))
                step(pool.tensor_tensor(t, e, e, ALU.mult))
                step(pool.tensor_scalar(p, t, ATANH[-1], None, ALU.mult))
                for c in ATANH[-2:0:-1]:
                    step(pool.tensor_scalar(p, p, c, None, ALU.add))
                    step(pool.tensor_tensor(p, p, t, ALU.mult))
                step(pool.tensor_scalar(p, p, ATANH[0], 2.0, ALU.add, ALU.mult))
                step(pool.tensor_tensor(p, p, e, ALU.mult))
                step(pool.tensor_scalar(v, v, 0.0, None, ALU.max))
                step(pool.tensor_tensor(dt, p, v, ALU.add))
                pool.wait_ge(nega_rdy, 1)
                step(pool.tensor_tensor(a, dt, per_head(neg_a[:, :]), ALU.mult))
                step(pool.tensor_copy(a_hl[:, half, :, 0, :], a))
                step(pool.tensor_tensor(a_hl[:, half, :, 1, :], a, a_hl[:, half, :, 0, :].bitcast(F32), ALU.subtract))
                assert done[0] == SOFT_STEPS * (half + 1)

            def out_weight_lo(v):
                pool.wait_ge(dhi, v + 1)
                pool.tensor_tensor(wo_lo[:, v, :], down_raw[:, v % 2, :], wo_hi[:, v, :].bitcast(F32), ALU.subtract)\
                    .then_inc(dlo, 1)

            def tri_times_a(n):
                half, c = divmod(n, CPH)
                pool.wait_ge(soft, SOFT_STEPS * (half + 1))
                wait(pool, e_ps, n)
                pool.tensor_tensor(
                    r_hl[:, :, :, :].rearrange("p s h q -> p (s h) q"),
                    tri[:, :].rearrange("p (a q) -> p a q", a=1).to_broadcast([P, 2 * H, P]),
                    a_hl[:, half, c, :, :].bitcast(F32).rearrange("p s (h a) -> p (s h) a", a=1)
                        .to_broadcast([P, 2 * H, P]),
                    ALU.mult).then_inc(r_rdy, 1)

            def decays(n):
                half, c = divmod(n, CPH)
                pool.wait_ge(dec_exp, n + 1)
                wait(pool, xs_rdy, n - 1)
                pool.tensor_tensor(to_end[:, n % 2, :], decay[:, :, P - 1], dt_c[:, half, c, :], ALU.mult)\
                    .then_inc(end_rdy, 1)
                pool.wait_ge(car_exp, n + 1)
                wait(pool, y_ps, n)
                pool.tensor_tensor(ce[:, :, :], carry[:, :, :],
                                   xbc[:, half, 2:CONV, c * P:(c + 1) * P], ALU.mult).then_inc(ce_rdy, 1)

            softplus(0)
            tri_times_a(0)
            out_weight_lo(0)
            out_weight_lo(1)
            tri_times_a(1)
            decays(0)
            out_weight_lo(2)
            out_weight_lo(3)
            for it in range(NCH + 1):
                if it + 2 < NCH:
                    tri_times_a(it + 2)
                if it + 1 < NCH:
                    decays(it + 1)
                if it == 1:
                    softplus(1)
                if 1 <= it:
                    rms_of(1, NCH + it - 1, hsq, it)
                    pool.wait_ge(hid_rdy, it)
                    pool.tensor_tensor(resid[:, it - 1, :], resid[:, it - 1, :], hid[:, :], ALU.add)\
                        .then_inc(hx_rdy, 1)

            for s in range(len(STAGES)):
                for t in range(CPH):
                    n = s * CPH + t
                    pool.wait_ge(mv_rdy, n + 1)
                    pool.tensor_scalar(rstd[:, t:t + 1], mv[:, t, 1:2], EPS, None, ALU.add)\
                        .then_inc(ve_rdy, 1)
                    on_act = s == len(STAGES) - 1 and t < CPH - 1
                    if on_act:
                        pool.tensor_scalar(shift[:, t:t + 1], mv[:, t, 0:1], -1.0, None, ALU.mult)\
                            .then_inc(minus_mean, 1)
                    pool.wait_ge(ve_rdy, n + 1)
                    pool.tensor_tensor(rstd[:, t:t + 1], rstd[:, t:t + 1], half_neg[:, :], ALU.pow)\
                        .then_inc(rstd_rdy, 1)
                    if on_act:
                        pool.wait_ge(minus_mean, t + 1)
                        pool.wait_ge(rstd_rdy, n + 1)
                        pool.tensor_tensor(shift[:, t:t + 1], shift[:, t:t + 1], rstd[:, t:t + 1], ALU.mult)\
                            .then_inc(shift_rdy, 1)

        @block.tensor
        def _(pe):
            def three(dst, w_hi, w_lo, m_hi, m_lo, start, stop):
                pe.matmul(dst, w_hi, m_hi, start=start, stop=False)
                pe.matmul(dst, w_hi, m_lo, start=False, stop=False)
                return pe.matmul(dst, w_lo, m_hi, start=False, stop=stop)

            def transpose_chunk(dst, src, signal):
                for k in range(KT):
                    last = pe.transpose(dst[:, k * P:(k + 1) * P], src[:, k * P:(k + 1) * P], ident[:, :])
                last.then_inc(signal, 1)

            def x_t(c):
                pe.wait_ge(xn_rdy, c + 1)
                if c >= CPH:
                    pe.wait_ge(xt_lo, max(CPH, c - 1))
                transpose_chunk(x_bank(c), normed[:, c % 2, :], xt_ps)

            def project(half, i):
                u, j = half * IN_PAIRS + i // 2, i % 2
                n = half * IN_COUNT + i
                if n == 0:
                    pe.wait_ge(first_lo, 1)
                    for part, b in enumerate(FIRST):
                        pe.wait_ge(xt_lo, CPH // 2 * (part + 1))
                        tok = slice(part * HT // 2, (part + 1) * HT // 2)
                        for k in range(KT):
                            last = three(b[:, 0:HT // 2], pair_hi[:, 0, 0, k, :], pair_lo[:, 0, 0, k, :],
                                         act_hi[:, 0, k, tok], act_lo[:, 0, k, tok], k == 0, k == KT - 1)
                    last.then_inc(in_ps, 1)
                    return
                pe.wait_ge(plo, u + 1)
                if half == 0:
                    wait(pe, in_free, n - 1)
                else:
                    former = [j for j in range(i) if BETWEEN_BANK[j] == BETWEEN_BANK[i]]
                    pe.wait_ge(in_free, IN_COUNT + (former[-1] + 1 if former else 0))
                for k in range(KT):
                    last = three(in_bank(half, i)[:, :], pair_hi[:, u % 2, j, k, :], pair_lo[:, u % 2, j, k, :],
                                 act_hi[:, half, k, :], act_lo[:, half, k, :], k == 0, k == KT - 1)
                last.then_inc(in_ps, 1)

            def dt_t(half):
                pe.wait_ge(in_free, half * IN_COUNT + 1)
                wait(pe, dec_exp, 2 * half)
                for c in range(CPH):
                    last = pe.transpose(B_D[:, c * P:(c + 1) * P], dt_row[:, c * P:(c + 1) * P], ident[:, :])
                last.then_inc(dtt_ps, 1)

            def bx_t(n):
                half, c = divmod(n, CPH)
                pe.wait_ge(conv_rdy, half * CONV + 2)
                if n == 0:
                    pe.wait_ge(in_free, IN_COUNT - 1)
                wait(pe, bx_rdy, n)
                for (it, _), i in BETWEEN.items():
                    if it == n - 2 and BETWEEN_BANK[i] == 1:
                        pe.wait_ge(in_free, IN_COUNT + i + 1)
                for i, tile in enumerate((1, 0)):
                    last = pe.transpose(B_BX[:, i * P:(i + 1) * P], xbc[:, half, tile, c * P:(c + 1) * P],
                                        ident[:, :])
                last.then_inc(bxt_ps, 1)

            def flat(t):
                return t.rearrange("p h q -> p (h q)")

            def scores(n):
                half, c = divmod(n, CPH)
                tok = slice(c * P, (c + 1) * P)
                wait(pe, dec_exp, n)
                if n == 0:
                    pe.wait_ge(dt_sum, 1)
                    pe.wait_ge(ones_rdy, 4)
                if n == 2:
                    pe.wait_ge(dt_sum, 3)
                pe.matmul(B_D[:, :], ident_r[:, :], flat(never[:, :, :]), start=True, stop=False)
                pe.wait_ge(r_rdy, n + 1)
                for i in range(2):
                    last = pe.matmul(B_D[:, :], strict[:, :], flat(r_hl[:, i, :, :]), start=False, stop=i == 1)
                last.then_inc(d_ps, 1)
                if n == 0:
                    pe.wait_ge(xt_lo, NCH)
                wait(pe, car_exp, n)
                for i in range(2):
                    last = pe.matmul(B_E[:, :], ones[:, :], flat(r_hl[:, i, :, :]), start=i == 0, stop=i == 1)
                last.then_inc(e_ps, 1)
                pe.wait_ge(conv_rdy, (half + 1) * CONV)
                wait(pe, att_mul, n)
                pe.matmul(B_S[:, :], xbc[:, half, 1, tok], xbc[:, half, 2:CONV, tok], start=True, stop=True)\
                    .then_inc(s_ps, 1)

            def mix(n):
                wait(pe, y_rdy, n)
                if n:
                    pe.wait_ge(ce_rdy, n + 1)
                    pe.wait_ge(st_rdy, n)
                    for h in range(H):
                        pe.matmul(B_Y[:, h * P:(h + 1) * P], state[:, h, :], ce[:, h, :],
                                  start=h == 0, stop=False, skip_group_check=True)
                pe.wait_ge(att_d, n + 1)
                pe.wait_ge(bx_rdy, n + 1)
                pe.matmul(B_Y[:, :], bx[:, n % 2, 1, :], flat(att[:, n % 2, :, :]), start=n == 0, stop=True,
                          skip_group_check=True).then_inc(y_ps, 1)
                if n < NCH - 1:
                    pe.wait_ge(xs_rdy, n + 1)
                    wait(pe, h2t_lo, n - 2)
                    pe.matmul(B_ST[:, :], bx[:, n % 2, 0, :], flat(xs[:, n % 2, :, :]), start=True, stop=True)\
                        .then_inc(st_ps, 1)

            def out_proj(n):
                if n == 0:
                    pe.wait_ge(dlo, H)
                pe.wait_ge(y_lo_s, n + 1)
                wait(pe, hid_rdy, n)
                for h in range(H):
                    last = three(B_O[:, :], y_hl[:, n % 2, 0, h, :], y_hl[:, n % 2, 1, h, :],
                                 wo_hi[:, h, :], wo_lo[:, h, :], h == 0, h == H - 1)
                last.then_inc(o_ps, 1)

            def h2_t(n):
                pe.wait_ge(h2_rdy, n + 1)
                pe.wait_ge(st_rdy, min(n + 3, NCH - 1))
                wait(pe, h2t_lo, n)
                transpose_chunk(B_ST, normed[:, n % 2, :], h2t_ps)

            def fill(it, place):
                if (it, place) in BETWEEN:
                    i = BETWEEN[it, place]
                    if BETWEEN_BANK[i] == 1:
                        pe.wait_ge(bx_rdy, it + 2)
                    project(1, i)

            pe.wait_ge(masks, 1)
            for _ in range(WARM_UP):
                pe.transpose(B_IN[1][:, 0:P], ident[:, :], ident[:, :])
            for c in range(CPH):
                x_t(c)
            for i in range(IN_COUNT):
                project(0, i)
                if i == 1:
                    dt_t(0)
                if i % 2 and i < 8:
                    x_t(CPH + i // 2)
            bx_t(0)
            scores(0)
            pe.wait_ge(xt_lo, NCH)
            fill(-1, 4)
            bx_t(1)
            for it in range(NCH):
                if it + 1 < NCH:
                    scores(it + 1)
                fill(it, 0)
                if it == 0:
                    dt_t(1)
                mix(it)
                fill(it, 1)
                if it >= 1:
                    out_proj(it - 1)
                fill(it, 2)
                if it >= 2:
                    h2_t(it - 2)
                fill(it, 3)
                fill(it, 4)
                if it + 2 < NCH:
                    bx_t(it + 2)

            def gate_up(i, c, half):
                pe.wait_ge(plo, i * 2 + (c + U0 + 1))
                for j, (freed, signal) in enumerate(((silu_rdy, gate_ps), (g_rdy, up_ps))):
                    if c == 0 and j == 0:
                        pe.wait_ge(in_free, NHALF * IN_COUNT)
                    elif c == 0:
                        pe.wait_ge(bx_rdy, NCH)
                    else:
                        pe.wait_ge(freed, i * 2 + c)
                    for k in range(KT):
                        last = three(B_IN[j][:, :], pair_hi[:, c % 2, j, k, :], pair_lo[:, c % 2, j, k, :],
                                     act_hi[:, half, k, :], act_lo[:, half, k, :], k == 0, k == KT - 1)
                    last.then_inc(signal, 1)

            def down(i, c, start, stop):
                pe.wait_ge(dlo, i * 2 + (c + H + 1))
                pe.wait_ge(g_lo_s, i * 2 + (c + 1))
                for t in range(CPH):
                    tok = slice(t * P, (t + 1) * P)
                    last = three(B_ACC[t][:, :], g_hl[c % 2][:, 0, tok], g_hl[c % 2][:, 1, tok],
                                 down_hi[:, c % 2, :], down_lo[:, c % 2, :], start, stop)
                    if stop and t < CPH - 1:
                        last.then_inc(acc_ps, 1)
                last.then_inc(down_used, 1)

            def ln_t(half, part):
                for t in (2 * part, 2 * part + 1):
                    n = half * CPH + t
                    pe.wait_ge(ln_rdy, n + 1)
                    wait(pe, lt_lo, n - 1)
                    transpose_chunk(B_NT[n % 2], resid[:, n, :], lt_ps)

            pe.wait_ge(h2t_lo, CPH)
            gate_up(0, 0, 0)
            h2_t(NCH - 2)
            out_proj(NCH - 1)
            for s, (p0, d0, n, half) in enumerate(STAGES):
                b = BASE[s]
                gate_up(0, b + 1, half)
                if s:
                    pe.wait_ge(acc_free, CPH * s)
                else:
                    h2_t(NCH - 1)
                    pe.wait_ge(y_rdy, NCH)
                down(0, b, True, False)
                for part, (first, end) in enumerate(loops(s)):
                    with pe.Fori(first, end) as i:
                        for j in range(2):
                            gate_up(i, b + 2 + j, half)
                            down(i, b + 1 + j, False, False)
                    if s in (1, 2) and part < 2:
                        ln_t(s - 1, part)
                for k in range(2 * end + 2, n):
                    gate_up(0, b + k, half)
                    down(0, b + k - 1, False, False)
                if s + 1 < len(STAGES):
                    if s:
                        pe.wait_ge(lt_lo, CPH * s)
                    else:
                        pe.wait_ge(h2t_lo, NCH)
                    gate_up(0, b + n, STAGES[s + 1][3])
                down(0, b + n - 1, False, True)

        @block.scalar
        def _(act):
            def split_pair(i, c):
                act.wait_ge(pair_in[c % 2], i * 16 + 16 * (c // 2 + 1))
                act.activation(pair_hi[:, c % 2, :, :, :].rearrange("p j k f -> p (j k f)"),
                               pair_raw[:, c % 2, :, :, :].rearrange("p j k f -> p (j k f)"), ACT.Copy)\
                    .then_inc(phi, 1)

            def split_down(i, c, dst):
                act.wait_ge(down_in[c % 2], i * 16 + 16 * (c // 2 + 1))
                act.activation(dst, down_raw[:, c % 2, :], ACT.Copy).then_inc(dhi, 1)

            def square(src, which, c, signal):
                wait(act, xsq, NCH * which)
                wait(act, signal, c)
                act.activation(junk[:, :], src, ACT.Square, accum_out=ssq[:, which, c:c + 1])\
                    .then_inc(signal, 1)

            def transposed_hi(ps, count, b, n, signal):
                half, c = divmod(n, CPH)
                act.wait_ge(ps, count)
                act.activation(act_hi[:, half, :, c * P:(c + 1) * P], heads(b), ACT.Copy).then_inc(signal, 1)

            def conv_silu(half, m):
                j = CONV_ORDER[m]
                act.wait_ge(tap_dve, HALO * (half * CONV + m + 1))
                act.activation(xbc[:, half, j, :], xbc[:, half, j, :], ACT.Silu).then_inc(conv_rdy, 1)

            def leave(half, i):
                n = half * IN_COUNT + i
                kind, j = IN_TILES[i]
                act.wait_ge(in_ps, n + 1)
                b = in_bank(half, i)
                if kind == "dt":
                    if half == 0:
                        for part, first in enumerate(FIRST):
                            last = act.activation(dt_row[:, part * HT // 2:(part + 1) * HT // 2],
                                                  first[:, 0:HT // 2], ACT.Copy)
                        last.then_inc(in_free, 1)
                    else:
                        act.wait_ge(dtt_ps, 1)
                        act.activation(dt_row[:, :], b[:, :], ACT.Copy).then_inc(in_free, 1)
                elif kind == "conv":
                    if half:
                        act.wait_ge(tap_dve, HALO * i)
                        act.activation(cin[:, j, 0:HALO], cin[:, j, HT:HT + HALO], ACT.Copy)\
                            .then_inc(halo_rdy, 1)
                        act.wait_ge(halo_rdy, i)
                    act.activation(cin[:, j, HALO:HALO + HT], b[:, :], ACT.Copy).then_inc(cin_rdy, 1)
                    act.activation(xbc[:, half, j, :], b[:, :], ACT.Identity,
                                   scale=cw[:, j, HALO:TAPS], bias=cb[:, j:j + 1]).then_inc(in_free, 1)
                else:
                    act.activation(zs[:, half, j, :], b[:, :], ACT.Silu).then_inc(in_free, 1)

                if i % 2 or i == IN_COUNT - 1:
                    split_pair(0, half * IN_PAIRS + i // 2 + 2)

            def dt_exps(half):
                act.wait_ge(dt_sum, 2 * half + 2)
                act.activation(dv[:, 1, :, :], dv[:, 1, :, :], ACT.Exp).then_inc(dt_exp, 1)

            def exps(n):
                act.wait_ge(d_ps, n + 1)
                wait(act, att_mul, n)
                wait(act, end_rdy, n)
                act.activation(decay[:, :, :], heads(B_D), ACT.Exp).then_inc(dec_exp, 1)
                act.wait_ge(e_ps, n + 1)
                wait(act, ce_rdy, n)
                act.activation(carry[:, :, :], heads(B_E), ACT.Exp).then_inc(car_pre, 1)
                act.wait_ge(car_pre, n + 1)
                wait(act, st_rdy, n - 1)
                act.activation(carry_last[:, n % 2, :], carry[:, :, P - 1], ACT.Copy).then_inc(car_exp, 1)

            def bx_copy(n):
                act.wait_ge(bxt_ps, n + 1)
                wait(act, y_ps, n - 1)
                wait(act, st_ps, n - 1)
                act.activation(bx[:, n % 2, :, :], B_BX[:, 0:2 * P].rearrange("p (i q) -> p i q", i=2), ACT.Copy)\
                    .then_inc(bx_rdy, 1)

            def scale_x(n):
                act.wait_ge(bx_rdy, n + 1)
                act.wait_ge(end_rdy, n + 1)
                wait(act, st_ps, n - 1)
                for h in range(H):
                    last = act.activation(xs[:, n % 2, h, :], bx[:, n % 2, 1, :], ACT.Copy,
                                          scale=to_end[:, n % 2, h:h + 1])
                last.then_inc(xs_rdy, 1)

            def y_hi(n):
                act.wait_ge(y_rdy, n + 1)
                wait(act, o_ps, n - 1)
                act.activation(y_hl[:, n % 2, 0, :, :], y[:, :, :], ACT.Copy).then_inc(y_hi_s, 1)

            def leave_between(it, place):
                if (it, place) in BETWEEN:
                    leave(1, BETWEEN[it, place])

            def h2_hi(n):
                transposed_hi(h2t_ps, n + 1, B_ST, n, h2t_hi)

            def square_hid(n):
                act.wait_ge(hid_rdy, n + 1)
                square(hid[:, :], 1, n, hsq)

            for c in range(CPH):
                act.wait_ge(x_in[c], 16)
                square(resid[:, c, :], 0, c, xsq)
            for c in range(CPH):
                transposed_hi(xt_ps, c + 1, x_bank(c), c, xt_hi)
                if c == 0:
                    act.wait_ge(pair_in[0], 16)
                    act.activation(pair_hi[:, 0, 0, :, :], pair_raw[:, 0, 0, :, :], ACT.Copy).then_inc(first_hi, 1)
            act.activation(pair_hi[:, 0, 1, :, :], pair_raw[:, 0, 1, :, :], ACT.Copy).then_inc(phi, 1)
            split_pair(0, 1)
            act.wait_ge(consts_in, CONSTS * 16)
            act.activation(neg_a[:, :], neg_a[:, :], ACT.Exp).then_inc(aexp_rdy, 1)
            for c in range(CPH, NCH):
                act.wait_ge(x_in[c], 16)
                square(resid[:, c, :], 0, c, xsq)
            for i in range(IN_COUNT):
                leave(0, i)
                if i == 3:
                    dt_exps(0)
                if IN_TILES[i] in (("z", 0), ("z", 1), ("z", 2)):
                    for m in (2 * IN_TILES[i][1], 2 * IN_TILES[i][1] + 1):
                        conv_silu(0, m)
                if i == 8:
                    split_down(0, 0, wo_hi[:, 0, :])
                    split_down(0, 1, wo_hi[:, 1, :])
                if i % 2 and i // 2 < CPH:
                    transposed_hi(xt_ps, CPH + i // 2 + 1, x_bank(CPH + i // 2), CPH + i // 2, xt_hi)
            exps(0)
            bx_copy(0)
            split_down(0, 2, wo_hi[:, 2, :])
            split_down(0, 3, wo_hi[:, 3, :])
            leave_between(-1, 4)
            scale_x(0)
            bx_copy(1)
            for it in range(NCH):
                if it + 1 < NCH:
                    exps(it + 1)
                leave_between(it, 0)
                if it + 1 < NCH - 1:
                    scale_x(it + 1)
                if it == 0:
                    dt_exps(1)
                if it == 2:
                    for m in range(CONV - 2):
                        conv_silu(1, m)
                leave_between(it, 1)
                if it == 2:
                    for m in range(CONV - 2, CONV):
                        conv_silu(1, m)
                y_hi(it)
                leave_between(it, 2)
                if it >= 1:
                    square_hid(it - 1)
                if it >= 2:
                    h2_hi(it - 2)
                leave_between(it, 3)
                leave_between(it, 4)
                if it + 2 < NCH:
                    bx_copy(it + 2)
                if it == 4:
                    split_down(0, H, down_hi[:, 0, :])

            def gated_step(i, c):
                act.wait_ge(gate_ps, i * 2 + (c + 1))
                if c:
                    act.wait_ge(g_rdy, i * 2 + c)
                act.activation(gate_s, B_IN[0][:, :], ACT.Silu).then_inc(silu_rdy, 1)
                if c < STEPS - 2:
                    act.wait_ge(up_ps, i * 2 + (c + 1))
                    split_pair(i, c + U0 + 2)
                act.wait_ge(g_rdy, i * 2 + (c + 1))
                act.activation(g_hl[c % 2][:, 0, :], gated, ACT.Copy).then_inc(g_hi_s, 1)
                if c < STEPS - 1:
                    if c:
                        act.wait_ge(down_used, i * 2 + c)
                    split_down(i, c + H + 1, down_hi[:, (c + 1) % 2, :])

            def ln_hi(half, part):
                for t in (2 * part, 2 * part + 1):
                    n = half * CPH + t
                    transposed_hi(lt_ps, n + 1, B_NT[n % 2], n, lt_hi)

            for s, (p0, d0, n, half) in enumerate(STAGES):
                b = BASE[s]
                if s == 0:
                    act.wait_ge(att_mul, NCH)
                    act.wait_ge(end_rdy, NCH)
                gated_step(0, b)
                if s == 0:
                    h2_hi(NCH - 2)
                    square_hid(NCH - 1)
                gated_step(0, b + 1)
                if s == 0:
                    h2_hi(NCH - 1)
                for part, (first, end) in enumerate(loops(s)):
                    with act.Fori(first, end) as i:
                        for j in range(2):
                            gated_step(i, b + 2 + j)
                    if s in (1, 2) and part < 2:
                        ln_hi(s - 1, part)
                for k in range(2 * end + 2, n):
                    gated_step(0, b + k)
            for t in range(CPH - 1):
                act.wait_ge(shift_rdy, t + 1)
                act.activation(resid[:, half * CPH + t, :], resid[:, half * CPH + t, :], ACT.Identity,
                               scale=rstd[:, t:t + 1], bias=shift[:, t:t + 1]).then_inc(act_ln_rdy, 1)

        @block.vector
        def _(dve):
            def f32(t):
                return t.bitcast(F32)

            def pair_rest(i, c):
                dve.wait_ge(phi, i * 2 + (c + 1))
                dve.tensor_tensor(pair_lo[:, c % 2, :, :, :].rearrange("p j k f -> p (j k f)"),
                                  pair_raw[:, c % 2, :, :, :].rearrange("p j k f -> p (j k f)"),
                                  f32(pair_hi[:, c % 2, :, :, :].rearrange("p j k f -> p (j k f)")),
                                  ALU.subtract).then_inc(plo, 1)

            def down_rest(i, c, hi, lo):
                dve.wait_ge(dhi, i * 2 + (c + 1))
                dve.tensor_tensor(lo, down_raw[:, c % 2, :], f32(hi), ALU.subtract).then_inc(dlo, 1)

            def x_norm(c):
                dve.wait_ge(rms_rdy, c + 1)
                if c == 0:
                    dve.wait_ge(ln1_in, 16)
                wait(dve, xt_ps, c - 1)
                dve.scalar_tensor_tensor(out=normed[:, c % 2, :], in0=resid[:, c, :], scalar=rms[:, 0, c:c + 1],
                                         in1=ln_b[:, :], op0=ALU.mult, op1=ALU.mult).then_inc(xn_rdy, 1)

            def transposed_lo(hi_signal, count, b, n, signal):
                half, c = divmod(n, CPH)
                tok = slice(c * P, (c + 1) * P)
                dve.wait_ge(hi_signal, count)
                dve.tensor_tensor(act_lo[:, half, :, tok], heads(b), f32(act_hi[:, half, :, tok]), ALU.subtract)\
                    .then_inc(signal, 1)

            def taps(half, m):
                j = CONV_ORDER[m]
                dve.wait_ge(in_free, half * IN_COUNT + m + 2)
                if half == 0 and m == 0:
                    dve.wait_ge(zeroed, 8)
                for k in range(HALO):
                    wait(dve, tap_dve, HALO * (half * CONV + m) + k)
                    dve.scalar_tensor_tensor(out=xbc[:, half, j, :], in0=cin[:, j, k:k + HT],
                                             scalar=cw[:, j, k:k + 1], in1=xbc[:, half, j, :],
                                             op0=ALU.mult, op1=ALU.add).then_inc(tap_dve, 1)

            def dt_bias_sum(half):
                dve.wait_ge(dtt_ps, half + 1)
                if half == 0:
                    dve.wait_ge(consts_in, CONSTS * 16)
                wait(dve, soft, SOFT_STEPS * half)
                v, e = dv[:, 0, :, :], dv[:, 1, :, :]
                dve.tensor_tensor(v, heads(B_D)[:, :, 0:H], per_head(dtb_b[:, :]), ALU.add).then_inc(dt_sum, 1)
                dve.wait_ge(dt_sum, 2 * half + 1)
                dve.scalar_tensor_tensor(out=e, in0=v, scalar=-1.0, in1=v, op0=ALU.mult, op1=ALU.min)\
                    .then_inc(dt_sum, 1)

            def attention(n):
                half, c = divmod(n, CPH)
                dve.wait_ge(s_ps, n + 1)
                dve.wait_ge(dec_exp, n + 1)
                if c == 0:
                    dve.wait_ge(soft, SOFT_STEPS * (half + 1))
                wait(dve, y_ps, n - 1)
                for h in range(H):
                    last = dve.scalar_tensor_tensor(out=att[:, n % 2, h, :], in0=B_S[:, h * P:(h + 1) * P],
                                                    scalar=dt_c[:, half, c, h:h + 1], in1=decay[:, h, :],
                                                    op0=ALU.mult, op1=ALU.mult)
                last.then_inc(att_mul, 1)
                dve.wait_ge(att_mul, n + 1)
                if n == 0:
                    dve.wait_ge(diag_rdy, 1)
                dve.tensor_tensor(att[:, n % 2, :, :], att[:, n % 2, :, :], dskip_diag[:, :, :], ALU.add)\
                    .then_inc(att_d, 1)

            def y_gate(n):
                half, c = divmod(n, CPH)
                dve.wait_ge(in_free, (half + 1) * IN_COUNT)
                dve.wait_ge(y_ps, n + 1)
                wait(dve, y_lo_s, n)
                dve.tensor_tensor(y[:, :, :], heads(B_Y), zs[:, half, :, c * P:(c + 1) * P], ALU.mult)\
                    .then_inc(y_rdy, 1)

            def y_rest(n):
                dve.wait_ge(y_hi_s, n + 1)
                dve.tensor_tensor(y_hl[:, n % 2, 1, :, :], y[:, :, :], f32(y_hl[:, n % 2, 0, :, :]), ALU.subtract)\
                    .then_inc(y_lo_s, 1)

            def update_state(n):
                dve.wait_ge(st_ps, n + 1)
                dve.wait_ge(car_exp, n + 1)
                wait(dve, st_rdy, n)
                for h in range(H):
                    last = dve.scalar_tensor_tensor(out=state[:, h, :], in0=state[:, h, :],
                                                    scalar=carry_last[:, n % 2, h:h + 1],
                                                    in1=B_ST[:, h * P:(h + 1) * P], op0=ALU.mult, op1=ALU.add)
                last.then_inc(st_rdy, 1)

            def hidden(n):
                dve.wait_ge(o_ps, n + 1)
                wait(dve, hx_rdy, n)
                wait(dve, hsq, n)
                wait(dve, h2_rdy, n)
                dve.tensor_tensor(hid[:, :], B_O[:, :], resid[:, n, :], ALU.add).then_inc(hid_rdy, 1)

            def h2_norm(n):
                dve.wait_ge(rms_rdy, NCH + n + 1)
                dve.wait_ge(ln2_in, 16)
                wait(dve, h2t_ps, n - 1)
                if n < 2:
                    dve.wait_ge(xt_ps, NCH)
                dve.scalar_tensor_tensor(out=normed[:, n % 2, :], in0=hid[:, :], scalar=rms[:, 1, n:n + 1],
                                         in1=ln_b[:, :], op0=ALU.mult, op1=ALU.mult).then_inc(h2_rdy, 1)

            def h2_lo(n):
                transposed_lo(h2t_hi, n + 1, B_ST, n, h2t_lo)

            def tiles_rest(it, place):
                i = BETWEEN.get((it, place), 0)
                if i % 2 or i == IN_COUNT - 1:
                    pair_rest(0, IN_PAIRS + i // 2 + 2)

            for c in range(CPH):
                x_norm(c)
            for c in range(CPH):
                transposed_lo(xt_hi, c + 1, x_bank(c), c, xt_lo)
            dve.wait_ge(plo, 1)
            pair_rest(0, 1)
            x_norm(CPH)
            x_norm(CPH + 1)
            dve.wait_ge(masks, 4)
            dve.tensor_copy(strict[:, :], strict_f[:, :]).then_inc(ones_rdy, 1)
            dve.tensor_copy(ident_r[:, :], ident[:, :]).then_inc(ones_rdy, 1)
            dve.tensor_scalar(ones[:, :], strict_f[:, :], 0.0, 1.0, ALU.mult, ALU.add).then_inc(ones_rdy, 1)
            dve.tensor_copy(never[:, :, :], never_f[:, :].rearrange("p (a q) -> p a q", a=1)
                            .to_broadcast([P, H, P])).then_inc(ones_rdy, 1)
            dve.wait_ge(aexp_rdy, 1)
            dve.tensor_scalar(neg_a[:, :], neg_a[:, :], -1.0, None, ALU.mult).then_inc(nega_rdy, 1)
            dve.wait_ge(nega_rdy, 1)
            for p in range(IN_PAIRS):
                if p == 0:
                    dt_bias_sum(0)
                if p >= 2:
                    pair_rest(0, p + 2)
                if 0 <= 2 * p - 1 < CONV:
                    taps(0, 2 * p - 1)
                if p < 2:
                    pair_rest(0, p + 2)
                if 2 * p < CONV:
                    taps(0, 2 * p)
                if p < CPH:
                    transposed_lo(xt_hi, CPH + p + 1, x_bank(CPH + p), CPH + p, xt_lo)
                if p < 2:
                    x_norm(CPH + p + 2)
            attention(0)
            for it in range(NCH):
                if it >= 2:
                    h2_norm(it - 2)
                if it == 2:
                    taps(1, 4)
                if it + 1 < NCH:
                    attention(it + 1)
                if it == 0:
                    taps(1, 0)
                    dt_bias_sum(1)
                elif it == 1:
                    taps(1, 2)
                elif it == 2:
                    taps(1, 5)
                tiles_rest(it, 0)
                y_gate(it)
                if it + 1 < NCH:
                    update_state(it)
                y_rest(it)
                if it == 1:
                    taps(1, 3)
                if it == 0:
                    taps(1, 1)
                if it >= 1:
                    hidden(it - 1)
                tiles_rest(it, 1)
                tiles_rest(it, 2)
                if it >= 2:
                    h2_lo(it - 2)
                tiles_rest(it, 3)
                tiles_rest(it, 4)
                if it == 4:
                    down_rest(0, H, down_hi[:, 0, :], down_lo[:, 0, :])

            def gated_step(i, c):
                dve.wait_ge(silu_rdy, i * 2 + (c + 1))
                dve.wait_ge(up_ps, i * 2 + (c + 1))
                if c:
                    dve.wait_ge(g_lo_s, i * 2 + c)
                dve.tensor_tensor(gated, B_IN[1][:, :], gate_s, ALU.mult).then_inc(g_rdy, 1)
                if c < STEPS - 2:
                    pair_rest(i, c + U0 + 2)
                dve.wait_ge(g_hi_s, i * 2 + (c + 1))
                dve.tensor_tensor(g_hl[c % 2][:, 1, :], gated, f32(g_hl[c % 2][:, 0, :]), ALU.subtract)\
                    .then_inc(g_lo_s, 1)
                if c < STEPS - 1:
                    down_rest(i, c + H + 1, down_hi[:, (c + 1) % 2, :], down_lo[:, (c + 1) % 2, :])

            def join(s, t):
                n = STAGES[s][3] * CPH + t
                if t < CPH - 1:
                    dve.wait_ge(acc_ps, s * (CPH - 1) + t + 1)
                else:
                    dve.wait_ge(down_used, BASE[s] + STAGES[s][2])
                dve.wait_ge(hx_rdy, NCH)
                dve.tensor_tensor(resid[:, n, :], B_ACC[t][:, :], resid[:, n, :], ALU.add).then_inc(acc_free, 1)

            def moments(s, t):
                count = s * CPH + t + 1
                dve.wait_ge(acc_free, count)
                dve.bn_stats(bn[:, t, :], resid[:, STAGES[s][3] * CPH + t, :]).then_inc(bn_rdy, 1)
                dve.wait_ge(bn_rdy, count)
                dve.bn_aggr(mv[:, t, :], bn[:, t, :]).then_inc(mv_rdy, 1)

            def ln_apply(s, t):
                n = STAGES[s][3] * CPH + t
                dve.wait_ge(rstd_rdy, s * CPH + t + 1)
                dve.tensor_scalar(resid[:, n, :], resid[:, n, :], mv[:, t, 0:1], rstd[:, t:t + 1],
                                  ALU.subtract, ALU.mult).then_inc(ln_rdy, 1)

            def ln_lo(half, part):
                for t in (2 * part, 2 * part + 1):
                    n = half * CPH + t
                    transposed_lo(lt_hi, n + 1, B_NT[n % 2], n, lt_lo)

            h2_norm(NCH - 2)
            for s, (p0, d0, n, half) in enumerate(STAGES):
                b = BASE[s]
                gated_step(0, b)
                if s:
                    for t in range(CPH):
                        join(s - 1, t)
                    for t in range(CPH):
                        moments(s - 1, t)
                else:
                    h2_lo(NCH - 2)
                    hidden(NCH - 1)
                    h2_norm(NCH - 1)
                gated_step(0, b + 1)
                if s:
                    for t in range(CPH):
                        ln_apply(s - 1, t)
                else:
                    h2_lo(NCH - 1)
                for part, (first, end) in enumerate(loops(s)):
                    with dve.Fori(first, end) as i:
                        for j in range(2):
                            gated_step(i, b + 2 + j)
                    if s in (1, 2) and part < 2:
                        ln_lo(s - 1, part)
                for k in range(2 * end + 2, n):
                    gated_step(0, b + k)
            join(s, 0)
            for t in range(CPH):
                if t + 1 < CPH:
                    join(s, t + 1)
                moments(s, t)
            ln_apply(s, CPH - 1)


def loops(s):
    pairs = (STAGES[s][2] - 2) // 2 - (s == len(STAGES) - 1)
    cuts = [0, pairs // 3, 2 * (pairs // 3), pairs] if s in (1, 2) else [0, pairs]
    return list(zip(cuts, cuts[1:]))


def _feature_tiles(w, tiles):
    padded = np.zeros((tiles * P, DM), w.dtype)
    padded[:w.shape[0]] = w
    return padded.reshape(tiles, P, KT, P).transpose(0, 3, 2, 1)


def _down_tiles(w, tiles):
    padded = np.zeros((tiles * P, DM), w.dtype)
    padded[:w.shape[1]] = w.T
    return padded.reshape(tiles, P, DM)


def kernel(**inputs):
    import concourse.bacc as bacc
    from concourse.bass_utils import run_bass_kernel_spmd

    a = {k[3:]: np.asarray(v) for k, v in inputs.items()}
    w_in = _feature_tiles(a["attn_w_in"], 11)
    row = {"z": 0, "conv": H, "dt": 10}
    blank = np.zeros_like(w_in[0])
    firsts = [blank if kind == "pad" else w_in[row[kind] + j] for kind, j in IN_TILES]
    projections = np.stack(firsts).reshape(IN_PAIRS, 2, P, KT, P)
    mlp = np.stack([_feature_tiles(a[f"attn_{n}_w"], T_MLP) for n in ("gate", "up")], axis=1)
    ffn = np.stack([_feature_tiles(a[f"ffn_W_{n}"], T_FFN) for n in ("gate", "up")], axis=1)
    arrays = {
        "x": a["attn_hidden_states"].reshape(NCH, P, DM),
        "pairs": np.concatenate([projections, mlp, ffn]).transpose(0, 2, 1, 3, 4),
        "downs": np.concatenate([_down_tiles(a["attn_w_out"], H), _down_tiles(a["attn_down_w"], T_MLP),
                                 _down_tiles(a["ffn_W_down"], T_FFN)]),
        "conv_w": a["attn_conv_w"].reshape(CONV, P, TAPS).transpose(1, 0, 2),
        "conv_b": a["attn_conv_b"].reshape(CONV, P).T,
        "a_log": a["attn_A_log"].reshape(1, H),
        "d_skip": a["attn_D"].reshape(1, H),
        "dt_bias": a["attn_dt_bias"].reshape(1, H),
        "ln1": a["attn_ln1_w"].reshape(1, DM),
        "ln2": a["attn_ln2_w"].reshape(1, DM),
    }
    arrays = {f"in_{k}": np.ascontiguousarray(v) for k, v in arrays.items()}
    nc = bacc.Bacc("TRN2", target_bir_lowering=False, num_devices=1)
    args = [nc.dram_tensor(k, v.shape, F32, kind="ExternalInput").ap() for k, v in arrays.items()]
    out = nc.dram_tensor("out", (NCH, P, DM), F32, kind="ExternalOutput").ap()
    build(nc, *args, out)
    result = run_bass_kernel_spmd(nc, [arrays], core_ids=[0])
    return result.results[0]["out"].reshape(1, L, DM)
```
